# Optimizing a Trainium2 kernel written in Bass

```python
import numpy as np
import jax
import jax.numpy as jnp

def _softmax(x, axis=-1):
    return jax.nn.softmax(x, axis=axis)

def _gelu(x):
    return jax.nn.gelu(x, approximate=True)

def _silu(x):
    return jax.nn.silu(x)

def _sigmoid(x):
    return jax.nn.sigmoid(x)

def _layernorm(x, axis=-1, eps=1e-05):
    m = jnp.mean(x, axis=axis, keepdims=True)
    v = jnp.var(x, axis=axis, keepdims=True)
    return (x - m) / jnp.sqrt(v + eps)

def _scatter_add(tgt, idx, src, axis=0):
    return tgt.at[idx].add(src)

def _segment_sum(src, seg, n):
    return jax.ops.segment_sum(src, seg, n)
kernel_name = 'mk_gnn_preln_d4_gnn_r16_d17e28'

def setup_inputs(seed: int=0):
    np.random.seed(seed)
    _w = jnp.asarray

    def _rec_inputs():
        import jax
        import jax.numpy as jnp
        _gk = jax.random.key(seed)
        x = -0.000202 + 1 * jax.random.normal(jax.random.fold_in(_gk, 1), (6250, 128), jnp.float32)
        src = jax.random.randint(jax.random.fold_in(_gk, 2), (200000,), 0, 6250, jnp.int32)
        dst = jax.random.randint(jax.random.fold_in(_gk, 3), (200000,), 0, 6250, jnp.int32)
        _o = jnp.argsort(dst, stable=True)
        src = src[_o]
        dst = dst[_o]
        edge_type_8 = jax.random.randint(jax.random.fold_in(_gk, 13), (200000,), 0, 8, jnp.int32)
        node_type_4 = jax.random.randint(jax.random.fold_in(_gk, 14), (6250,), 0, 4, jnp.int32)
        return (x, src, dst, edge_type_8, node_type_4)
    x, src, dst, edge_type_8, node_type_4 = _rec_inputs()

    def _L0_gnn_setup():
        import jax, jax.numpy as jnp
        import numpy as np
        N, E, T, R, IN, H, D = (3125, 31250, 4, 8, 128, 4, 32)
        LAM = 0.3

        def _typed_linear(x, W, t):
            all_out = jnp.einsum('ni,tio->nto', x, W)
            return jnp.take_along_axis(all_out, t[:, None, None], axis=1)[:, 0]
        key = jax.random.key(seed)
        ks = jax.random.split(key, 16)
        s = 0.05
        inp = {'x': jax.random.normal(ks[0], (N, IN), dtype=jnp.float32), 'W_k': jax.random.normal(ks[1], (T, IN, H * D), dtype=jnp.float32) * s, 'W_q': jax.random.normal(ks[2], (T, IN, H * D), dtype=jnp.float32) * s, 'W_v': jax.random.normal(ks[3], (T, IN, H * D), dtype=jnp.float32) * s, 'W_pre': jax.random.normal(ks[4], (T, IN, H * D), dtype=jnp.float32) * s, 'W_a': jax.random.normal(ks[5], (T, H * D, H * D), dtype=jnp.float32) * s, 'rel_att': jax.random.normal(ks[6], (H, R, D, D), dtype=jnp.float32) * s, 'rel_msg': jax.random.normal(ks[7], (H, R, D, D), dtype=jnp.float32) * s, 'rel_pri': jnp.ones((H, R), dtype=jnp.float32), 'skip': jnp.ones((T,), dtype=jnp.float32), 'ntype': jax.random.randint(ks[8], (N,), 0, T), 'etype': jax.random.randint(ks[9], (E,), 0, R), 'src': jax.random.randint(ks[10], (E,), 0, N), 'dst': jax.random.randint(ks[11], (E,), 0, N)}
        return inp
    _L0_gnn_all = _L0_gnn_setup()
    _L0_gnn_in = {k: v for k, v in _L0_gnn_all.items() if k in ('W_k', 'W_q', 'W_v', 'W_pre', 'W_a', 'rel_att', 'rel_msg', 'rel_pri', 'skip')}
    del _L0_gnn_all

    def _L1_gnn_setup():
        import jax, jax.numpy as jnp
        import numpy as np
        N = 3125
        E = 50000
        DIN = 128
        H = 4
        C = 32
        EPS = 1e-05
        NEG_SLOPE = 0.2

        def layer_norm(x, g, b):
            m = jnp.mean(x, axis=-1, keepdims=True)
            v = jnp.mean((x - m) ** 2, axis=-1, keepdims=True)
            return (x - m) * jax.lax.rsqrt(v + EPS) * g + b

        def gat_conv(h, src, dst, W, att_src, att_dst, gat_b, n):
            xh = (h @ W).reshape(n, H, C)
            a_src = jnp.einsum('nhc,hc->nh', xh, att_src)
            a_dst = jnp.einsum('nhc,hc->nh', xh, att_dst)
            alpha = jax.nn.leaky_relu(a_src[src] + a_dst[dst], NEG_SLOPE)
            amax = jax.ops.segment_max(alpha, dst, num_segments=n)
            alpha = jnp.exp(alpha - amax[dst])
            denom = jax.ops.segment_sum(alpha, dst, num_segments=n)
            alpha = alpha / denom[dst]
            msg = xh[src] * alpha[:, :, None]
            out = jax.ops.segment_sum(msg, dst, num_segments=n)
            return out.reshape(n, H * C) + gat_b
        key = jax.random.key(seed)
        ks = jax.random.split(key, 14)
        s = 1.0 / np.sqrt(DIN)
        return {'x': jax.random.normal(ks[0], (N, DIN), dtype=jnp.float32), 'edge_index': jax.random.randint(ks[1], (2, E), 0, N, dtype=jnp.int64), 'ln1_g': jnp.ones((DIN,), jnp.float32), 'ln1_b': jnp.zeros((DIN,), jnp.float32), 'W': jax.random.normal(ks[2], (DIN, H * C), jnp.float32) * s, 'att_src': jax.random.normal(ks[3], (H, C), jnp.float32) * (1.0 / np.sqrt(C)), 'att_dst': jax.random.normal(ks[4], (H, C), jnp.float32) * (1.0 / np.sqrt(C)), 'gat_b': jnp.zeros((H * C,), jnp.float32), 'ln2_g': jnp.ones((H * C,), jnp.float32), 'ln2_b': jnp.zeros((H * C,), jnp.float32), 'w1': jax.random.normal(ks[5], (H * C, 2 * H * C), jnp.float32) * (1.0 / np.sqrt(H * C)), 'b1': jnp.zeros((2 * H * C,), jnp.float32), 'w2': jax.random.normal(ks[6], (2 * H * C, H * C), jnp.float32) * (1.0 / np.sqrt(2 * H * C)), 'b2': jnp.zeros((H * C,), jnp.float32)}
    _L1_gnn_all = _L1_gnn_setup()
    _L1_gnn_in = {k: v for k, v in _L1_gnn_all.items() if k in ('ln1_g', 'ln1_b', 'W', 'att_src', 'att_dst', 'gat_b', 'ln2_g', 'ln2_b', 'w1', 'b1', 'w2', 'b2')}
    del _L1_gnn_all

    def _L2_gnn_setup():
        import jax, jax.numpy as jnp
        import numpy as np
        N_NODES = 3125
        N_EDGES = 37500
        IN_FEATS = 128
        OUT_FEATS = 128
        key = jax.random.key(seed)
        k1, k2, k3, k4 = jax.random.split(key, 4)
        feat = jax.random.normal(k1, (N_NODES, IN_FEATS), dtype=jnp.float32)
        src = jax.random.randint(k2, (N_EDGES,), 0, N_NODES, dtype=jnp.int64)
        dst = jax.random.randint(k3, (N_EDGES,), 0, N_NODES, dtype=jnp.int64)
        limit = float(np.sqrt(6.0 / (IN_FEATS + OUT_FEATS)))
        weight = jax.random.uniform(k4, (IN_FEATS, OUT_FEATS), dtype=jnp.float32, minval=-limit, maxval=limit)
        bias = jnp.zeros((OUT_FEATS,), dtype=jnp.float32)
        return {'feat': feat, 'src': src, 'dst': dst, 'weight': weight, 'bias': bias}
    _L2_gnn_all = _L2_gnn_setup()
    _L2_gnn_in = {k: v for k, v in _L2_gnn_all.items() if k in ('weight', 'bias')}
    del _L2_gnn_all

    def _L3_gnn_setup():
        import jax, jax.numpy as jnp
        import numpy as np
        N_NODES = 6250
        N_EDGES = 100000
        D_MODEL = 128
        N_HEADS = 8
        D_HEAD = D_MODEL // N_HEADS

        def _batch_norm(x, w, b, eps=1e-05):
            m = x.mean(axis=0)
            v = x.var(axis=0)
            return (x - m) * jax.lax.rsqrt(v + eps) * w + b
        key = jax.random.key(seed)
        ks = jax.random.split(key, 12)
        s = 0.05
        inp = {'h': jax.random.normal(ks[0], (N_NODES, D_MODEL), dtype=jnp.float32), 'src': jax.random.randint(ks[1], (N_EDGES,), 0, N_NODES, dtype=jnp.int32), 'dst': jax.random.randint(ks[2], (N_EDGES,), 0, N_NODES, dtype=jnp.int32), 'Wq': jax.random.normal(ks[3], (D_MODEL, D_MODEL), dtype=jnp.float32) * s, 'Wk': jax.random.normal(ks[4], (D_MODEL, D_MODEL), dtype=jnp.float32) * s, 'Wv': jax.random.normal(ks[5], (D_MODEL, D_MODEL), dtype=jnp.float32) * s, 'Wo': jax.random.normal(ks[6], (D_MODEL, D_MODEL), dtype=jnp.float32) * s, 'bo': jnp.zeros((D_MODEL,), dtype=jnp.float32), 'W1': jax.random.normal(ks[7], (2 * D_MODEL, D_MODEL), dtype=jnp.float32) * s, 'b1': jnp.zeros((2 * D_MODEL,), dtype=jnp.float32), 'W2': jax.random.normal(ks[8], (D_MODEL, 2 * D_MODEL), dtype=jnp.float32) * s, 'b2': jnp.zeros((D_MODEL,), dtype=jnp.float32), 'bn1_w': jnp.ones((D_MODEL,), dtype=jnp.float32), 'bn1_b': jnp.zeros((D_MODEL,), dtype=jnp.float32), 'bn2_w': jnp.ones((D_MODEL,), dtype=jnp.float32), 'bn2_b': jnp.zeros((D_MODEL,), dtype=jnp.float32)}
        return inp
    _L3_gnn_all = _L3_gnn_setup()
    _L3_gnn_in = {k: v for k, v in _L3_gnn_all.items() if k in ('Wq', 'Wk', 'Wv', 'Wo', 'bo', 'W1', 'b1', 'W2', 'b2', 'bn1_w', 'bn1_b', 'bn2_w', 'bn2_b')}
    del _L3_gnn_all
    return {'x': x, 'src': src, 'dst': dst, 'edge_type_8': edge_type_8, 'node_type_4': node_type_4, 'L0_gnn_W_k': _L0_gnn_in['W_k'], 'L0_gnn_W_q': _L0_gnn_in['W_q'], 'L0_gnn_W_v': _L0_gnn_in['W_v'], 'L0_gnn_W_pre': _L0_gnn_in['W_pre'], 'L0_gnn_W_a': _L0_gnn_in['W_a'], 'L0_gnn_rel_att': _L0_gnn_in['rel_att'], 'L0_gnn_rel_msg': _L0_gnn_in['rel_msg'], 'L0_gnn_rel_pri': _L0_gnn_in['rel_pri'], 'L0_gnn_skip': _L0_gnn_in['skip'], 'L1_gnn_ln1_g': _L1_gnn_in['ln1_g'], 'L1_gnn_ln1_b': _L1_gnn_in['ln1_b'], 'L1_gnn_W': _L1_gnn_in['W'], 'L1_gnn_att_src': _L1_gnn_in['att_src'], 'L1_gnn_att_dst': _L1_gnn_in['att_dst'], 'L1_gnn_gat_b': _L1_gnn_in['gat_b'], 'L1_gnn_ln2_g': _L1_gnn_in['ln2_g'], 'L1_gnn_ln2_b': _L1_gnn_in['ln2_b'], 'L1_gnn_w1': _L1_gnn_in['w1'], 'L1_gnn_b1': _L1_gnn_in['b1'], 'L1_gnn_w2': _L1_gnn_in['w2'], 'L1_gnn_b2': _L1_gnn_in['b2'], 'L2_gnn_weight': _L2_gnn_in['weight'], 'L2_gnn_bias': _L2_gnn_in['bias'], 'L3_gnn_Wq': _L3_gnn_in['Wq'], 'L3_gnn_Wk': _L3_gnn_in['Wk'], 'L3_gnn_Wv': _L3_gnn_in['Wv'], 'L3_gnn_Wo': _L3_gnn_in['Wo'], 'L3_gnn_bo': _L3_gnn_in['bo'], 'L3_gnn_W1': _L3_gnn_in['W1'], 'L3_gnn_b1': _L3_gnn_in['b1'], 'L3_gnn_W2': _L3_gnn_in['W2'], 'L3_gnn_b2': _L3_gnn_in['b2'], 'L3_gnn_bn1_w': _L3_gnn_in['bn1_w'], 'L3_gnn_bn1_b': _L3_gnn_in['bn1_b'], 'L3_gnn_bn2_w': _L3_gnn_in['bn2_w'], 'L3_gnn_bn2_b': _L3_gnn_in['bn2_b']}

def reference(x, src, dst, edge_type_8, node_type_4, L0_gnn_W_k, L0_gnn_W_q, L0_gnn_W_v, L0_gnn_W_pre, L0_gnn_W_a, L0_gnn_rel_att, L0_gnn_rel_msg, L0_gnn_rel_pri, L0_gnn_skip, L1_gnn_ln1_g, L1_gnn_ln1_b, L1_gnn_W, L1_gnn_att_src, L1_gnn_att_dst, L1_gnn_gat_b, L1_gnn_ln2_g, L1_gnn_ln2_b, L1_gnn_w1, L1_gnn_b1, L1_gnn_w2, L1_gnn_b2, L2_gnn_weight, L2_gnn_bias, L3_gnn_Wq, L3_gnn_Wk, L3_gnn_Wv, L3_gnn_Wo, L3_gnn_bo, L3_gnn_W1, L3_gnn_b1, L3_gnn_W2, L3_gnn_b2, L3_gnn_bn1_w, L3_gnn_bn1_b, L3_gnn_bn2_w, L3_gnn_bn2_b):
    import jax
    import jax.numpy as jnp

    def _L0_gnn_ref(x, W_k, W_q, W_v, W_pre, W_a, rel_att, rel_msg, rel_pri, skip, ntype, etype, src, dst):
        import jax, jax.numpy as jnp
        import numpy as np
        N, E, T, R, IN, H, D = (3125, 31250, 4, 8, 128, 4, 32)
        LAM = 0.3

        def _typed_linear(x, W, t):
            all_out = jnp.einsum('ni,tio->nto', x, W)
            return jnp.take_along_axis(all_out, t[:, None, None], axis=1)[:, 0]
        n = x.shape[0]
        sqrt_d = jnp.asarray(np.sqrt(D), dtype=x.dtype)
        k = _typed_linear(x, W_k, ntype).reshape(n, H, D)
        q = _typed_linear(x, W_q, ntype).reshape(n, H, D)
        v = _typed_linear(x, W_v, ntype).reshape(n, H, D)
        k_e = k[src]
        q_e = q[dst]
        v_e = v[src]
        kw = jnp.zeros_like(k_e)
        msg = jnp.zeros_like(v_e)
        for r in range(R):
            sel = (etype == r)[:, None, None].astype(x.dtype)
            kw = kw + sel * jnp.einsum('ehd,hdf->ehf', k_e, rel_att[:, r])
            msg = msg + sel * jnp.einsum('ehd,hdf->ehf', v_e, rel_msg[:, r])
        pri = rel_pri.T[etype]
        a = (kw * q_e).sum(-1) * pri / sqrt_d
        amax = jax.ops.segment_max(a, dst, num_segments=n)
        ex = jnp.exp(a - amax[dst])
        denom = jax.ops.segment_sum(ex, dst, num_segments=n)
        att = ex / denom[dst]
        agg = jax.ops.segment_sum(msg * att[..., None], dst, num_segments=n)
        pre = _typed_linear(x, W_pre, ntype).reshape(n, H, D)
        h = (LAM * agg + (1.0 - LAM) * pre).reshape(n, H * D)
        h = _typed_linear(h, W_a, ntype)
        alpha = jax.nn.sigmoid(skip[ntype])[:, None]
        return h * alpha + x * (1.0 - alpha)

    def _L1_gnn_ref(x, edge_index, ln1_g, ln1_b, W, att_src, att_dst, gat_b, ln2_g, ln2_b, w1, b1, w2, b2):
        import jax, jax.numpy as jnp
        import numpy as np
        N = 3125
        E = 50000
        DIN = 128
        H = 4
        C = 32
        EPS = 1e-05
        NEG_SLOPE = 0.2

        def layer_norm(x, g, b):
            m = jnp.mean(x, axis=-1, keepdims=True)
            v = jnp.mean((x - m) ** 2, axis=-1, keepdims=True)
            return (x - m) * jax.lax.rsqrt(v + EPS) * g + b

        def gat_conv(h, src, dst, W, att_src, att_dst, gat_b, n):
            xh = (h @ W).reshape(n, H, C)
            a_src = jnp.einsum('nhc,hc->nh', xh, att_src)
            a_dst = jnp.einsum('nhc,hc->nh', xh, att_dst)
            alpha = jax.nn.leaky_relu(a_src[src] + a_dst[dst], NEG_SLOPE)
            amax = jax.ops.segment_max(alpha, dst, num_segments=n)
            alpha = jnp.exp(alpha - amax[dst])
            denom = jax.ops.segment_sum(alpha, dst, num_segments=n)
            alpha = alpha / denom[dst]
            msg = xh[src] * alpha[:, :, None]
            out = jax.ops.segment_sum(msg, dst, num_segments=n)
            return out.reshape(n, H * C) + gat_b
        n = x.shape[0]
        loops = jnp.arange(n, dtype=edge_index.dtype)
        src = jnp.concatenate([edge_index[0], loops])
        dst = jnp.concatenate([edge_index[1], loops])
        h = layer_norm(x, ln1_g, ln1_b)
        h = gat_conv(h, src, dst, W, att_src, att_dst, gat_b, n)
        h = h + x
        hn = layer_norm(h, ln2_g, ln2_b)
        ffn = jax.nn.gelu(hn @ w1 + b1, approximate=False) @ w2 + b2
        return h + ffn

    def _L2_gnn_ref(feat, src, dst, weight, bias):
        import jax, jax.numpy as jnp
        import numpy as np
        N_NODES = 3125
        N_EDGES = 37500
        IN_FEATS = 128
        OUT_FEATS = 128
        n = feat.shape[0]
        ones = jnp.ones(src.shape, feat.dtype)
        out_deg = jnp.clip(jax.ops.segment_sum(ones, src, num_segments=n), 1.0)
        in_deg = jnp.clip(jax.ops.segment_sum(ones, dst, num_segments=n), 1.0)
        h = feat * (out_deg ** (-0.5))[:, None]
        agg = jax.ops.segment_sum(h[src], dst, num_segments=n)
        rst = agg @ weight
        rst = rst * (in_deg ** (-0.5))[:, None]
        rst = rst + bias
        return jax.nn.relu(rst)

    def _L3_gnn_ref(h, src, dst, Wq, Wk, Wv, Wo, bo, W1, b1, W2, b2, bn1_w, bn1_b, bn2_w, bn2_b):
        import jax, jax.numpy as jnp
        import numpy as np
        N_NODES = 6250
        N_EDGES = 100000
        D_MODEL = 128
        N_HEADS = 8
        D_HEAD = D_MODEL // N_HEADS

        def _batch_norm(x, w, b, eps=1e-05):
            m = x.mean(axis=0)
            v = x.var(axis=0)
            return (x - m) * jax.lax.rsqrt(v + eps) * w + b
        N = h.shape[0]
        Q = (h @ Wq.T).reshape(N, N_HEADS, D_HEAD)
        K = (h @ Wk.T).reshape(N, N_HEADS, D_HEAD)
        V = (h @ Wv.T).reshape(N, N_HEADS, D_HEAD)
        score = jnp.einsum('ehd,ehd->eh', K[src], Q[dst]) / np.sqrt(D_HEAD).astype(np.float32)
        s = jnp.exp(jnp.clip(score, -5.0, 5.0))[:, :, None]
        wV = jax.ops.segment_sum(V[src] * s, dst, num_segments=N)
        z = jax.ops.segment_sum(s, dst, num_segments=N)
        h_attn = (wV / (z + 1e-06)).reshape(N, D_MODEL)
        x = h_attn @ Wo.T + bo
        x = h + x
        x = _batch_norm(x, bn1_w, bn1_b)
        y = jax.nn.relu(x @ W1.T + b1) @ W2.T + b2
        y = x + y
        y = _batch_norm(y, bn2_w, bn2_b)
        return y
    edge_index = jnp.stack([src, dst])
    h = jnp.maximum(_layernorm(x, axis=-1), 0.0)
    x = x + _L0_gnn_ref(h, L0_gnn_W_k, L0_gnn_W_q, L0_gnn_W_v, L0_gnn_W_pre, L0_gnn_W_a, L0_gnn_rel_att, L0_gnn_rel_msg, L0_gnn_rel_pri, L0_gnn_skip, node_type_4, edge_type_8, src, dst)
    h = jnp.maximum(_layernorm(x, axis=-1), 0.0)
    x = x + _L1_gnn_ref(h, edge_index, L1_gnn_ln1_g, L1_gnn_ln1_b, L1_gnn_W, L1_gnn_att_src, L1_gnn_att_dst, L1_gnn_gat_b, L1_gnn_ln2_g, L1_gnn_ln2_b, L1_gnn_w1, L1_gnn_b1, L1_gnn_w2, L1_gnn_b2)
    h = jnp.maximum(_layernorm(x, axis=-1), 0.0)
    x = x + _L2_gnn_ref(h, src, dst, L2_gnn_weight, L2_gnn_bias)
    h = jnp.maximum(_layernorm(x, axis=-1), 0.0)
    x = x + _L3_gnn_ref(h, src, dst, L3_gnn_Wq, L3_gnn_Wk, L3_gnn_Wv, L3_gnn_Wo, L3_gnn_bo, L3_gnn_W1, L3_gnn_b1, L3_gnn_W2, L3_gnn_b2, L3_gnn_bn1_w, L3_gnn_bn1_b, L3_gnn_bn2_w, L3_gnn_bn2_b)
    return x

_drawn_inputs = setup_inputs


def setup_inputs(seed=0):
    import zlib

    import numpy as np

    out = dict(_drawn_inputs(seed))
    spreads = {'L0_gnn_rel_pri': (1.0, 0.6),
     'L0_gnn_skip': (1.0, 0.6),
     'L1_gnn_ln1_g': (1.0, 0.2),
     'L1_gnn_ln1_b': (0.0, 0.1),
     'L1_gnn_gat_b': (0.0, 0.1),
     'L1_gnn_ln2_g': (1.0, 0.2),
     'L1_gnn_ln2_b': (0.0, 0.28),
     'L1_gnn_b1': (0.0, 0.307),
     'L1_gnn_b2': (0.0, 0.1),
     'L2_gnn_bias': (0.0, 0.36),
     'L3_gnn_bo': (0.0, 2.0),
     'L3_gnn_b1': (0.0, 0.563),
     'L3_gnn_b2': (0.0, 2.0),
     'L3_gnn_bn1_w': (1.0, 0.556),
     'L3_gnn_bn1_b': (0.0, 0.8),
     'L3_gnn_bn2_w': (1.0, 0.2),
     'L3_gnn_bn2_b': (0.0, 0.1)}
    factors = {'L0_gnn_W_k': 8.0,
     'L0_gnn_W_q': 8.0,
     'L0_gnn_W_v': 8.0,
     'L0_gnn_rel_att': 8.0,
     'L0_gnn_rel_msg': 8.0,
     'L3_gnn_Wq': 8.0,
     'L3_gnn_Wk': 8.0}
    for name, (base, spread) in spreads.items():
        noise = np.random.default_rng([zlib.crc32(name.encode()), seed]).standard_normal(out[name].shape)
        drawn = base * np.exp(spread * noise) if base else spread * noise
        out[name] = jnp.asarray(drawn.astype(out[name].dtype))
    for name, factor in factors.items():
        out[name] = (out[name] * factor).astype(out[name].dtype)
    return out
```

```python
from contextlib import ExitStack, contextmanager

import numpy as np

import concourse.bass as bass
from concourse import mybir

ALU = mybir.AluOpType
ACT = mybir.ActivationFunctionType
AX = mybir.AxisListType
F32 = mybir.dt.float32
BF16 = mybir.dt.bfloat16
I32 = mybir.dt.int32

P = 128
N = 6250
NT = -(-N // P)
NP = NT * P
TAIL = N - (NT - 1) * P
E = 200000
G = 4
GE = G * P
NG = -(-E // GE)
NV = -(-(NG + NT - 1) // G) * G
VC = 4
VP = NV // VC
D = 128
R = 8
T = 4
BIG = 1e30
LN_EPS = 1e-5
LAM = 0.3
SLOPE = 0.2


def bcast(ap, shape):
    return ap.unsqueeze(len(ap.shape)).broadcast_to(shape)


class Phase:

    def __init__(self, nc, name, ctx):
        self.nc, self.name, self.ctx, self.sems = nc, name, ctx, []

    def sb(self, name, shape, dt=F32):
        return self.ctx.enter_context(self.nc.sbuf_tensor(f"{self.name}_{name}", shape, dt))

    def ps(self, name, shape, dt=F32):
        return self.ctx.enter_context(self.nc.psum_tensor(f"{self.name}_{name}", shape, dt))

    def sem(self, name):
        self.sems.append(self.nc.alloc_semaphore(f"{self.name}_{name}"))
        return self.sems[-1]


@contextmanager
def phase(nc, name):
    with ExitStack() as ctx:
        p = Phase(nc, name, ctx)
        yield p
    nc.clear_and_free_semaphores(p.sems)
    nc.all_engine_barrier()


class Chain:

    def __init__(self, eng, sem):
        self.eng, self.sem, self.n = eng, sem, 0

    def __call__(self, ins):
        self.n += 1
        ins.then_inc(self.sem, 1)
        self.eng.wait_ge(self.sem, self.n)


def node_tiles(eng, body):
    body(0, 0, 0)
    body(1, 1, 0)
    with eng.Fori(1, NT // 2) as i:
        body(i * 2, 0, i)
        body(i * 2 + 1, 1, i)
    body(NT - 1, 0, NT // 2)


def known(t, least):
    return not isinstance(t, int) or t >= least


class LayerNorm:

    def __init__(self, p, x, out, square, relu, gamma=None, beta=None):
        self.x, self.out, self.square, self.relu, self.gamma, self.beta = x, out, square, relu, gamma, beta
        self.mean, self.var, self.rstd = (p.sb(n, [P, NT]) for n in ("mean", "var", "rstd"))
        self.centred, self.squared, self.var_ready, self.std_ready, self.steps, self.done = (
            p.sem(n) for n in ("ln_centred", "ln_squared", "ln_var", "ln_std", "ln_steps", "ln_done"))

    def vector(self, nc, dve):
        link = Chain(dve, self.steps)
        shape = [P, NT, D]
        link(nc.vector.reduce_sum(self.mean[:], self.x, AX.X))
        link(nc.vector.tensor_scalar(self.mean[:], self.mean[:], 1.0 / D, None, ALU.mult))
        nc.vector.tensor_tensor(self.out, self.x, bcast(self.mean[:], shape), ALU.subtract).then_inc(self.centred, 1)
        dve.wait_ge(self.squared, 1)
        link(nc.vector.reduce_sum(self.var[:], self.square, AX.X))
        nc.vector.tensor_scalar(self.var[:], self.var[:], 1.0 / D, LN_EPS, ALU.mult, ALU.add).then_inc(self.var_ready, 1)
        dve.wait_ge(self.std_ready, 1)
        link(nc.vector.reciprocal(self.rstd[:], self.var[:]))
        if self.relu:
            link(nc.vector.tensor_scalar(self.out, self.out, 0.0, None, ALU.max))
        last = nc.vector.tensor_tensor(self.out, self.out, bcast(self.rstd[:], shape), ALU.mult)
        if self.gamma is not None:
            link(last)
            rows = [P, NT, D]
            link(nc.vector.tensor_tensor(self.out, self.out, self.gamma.unsqueeze(1).broadcast_to(rows), ALU.mult))
            last = nc.vector.tensor_tensor(self.out, self.out, self.beta.unsqueeze(1).broadcast_to(rows), ALU.add)
        last.then_inc(self.done, 1)

    def scalar(self, nc, act):
        act.wait_ge(self.centred, 1)
        nc.scalar.activation(self.square, self.out, ACT.Square).then_inc(self.squared, 1)
        act.wait_ge(self.var_ready, 1)
        nc.scalar.activation(self.var[:], self.var[:], ACT.Sqrt).then_inc(self.std_ready, 1)


def plan_visits(nc, c, edge, dram, res):
    with phase(nc, "plan") as p:
        ends_i, ends_b, ends_f = p.sb("ends_i", [1, 2, NG], I32), p.sb("ends_b", [1, 2, NG], I32), p.sb("ends_f", [1, 2, NG])
        ones_row = p.sb("ones_row", [1, P])
        blk_first, n_blocks, csum, base, ones_g, junk = (
            p.sb(n, [P, NG]) for n in ("blk_first", "n_blocks", "csum", "base", "ones_g", "junk"))
        vis, tv, bv, shift = (p.sb(n, [VP, VC]) for n in ("vis", "tv", "bv", "shift"))
        tvi, bvi = p.sb("tvi", [VP, VC], I32), p.sb("bvi", [VP, VC], I32)
        git = p.sb("git", [P, NG])
        dst_g, src_g, et_g = (p.sb(n, [VP, VC, GE], I32) for n in ("dst_g", "src_g", "et_g"))
        dl = p.sb("dl", [VP, GE])
        sq, hi, lo = (p.sb(n, [VP, GE], I32) for n in ("sq", "hi", "lo"))
        feat = p.sb("feat", [VP, 2, 5, GE], BF16)
        flag, last, ia, ib = (p.sb(n, [VP, 2, GE]) for n in ("flag", "last", "ia", "ib"))
        ps_first, ps_last = p.ps("ps_first", [P, 512]), p.ps("ps_last", [P, 512])
        ps_t = [p.ps(n, [P, G, VP]) for n in ("ps_ta", "ps_tb", "ps_tc")]
        lo_i, hi_i, his = p.sb("lo_i", [P, NG * G + G], I32), p.sb("hi_i", [P, NG * G + G], I32), p.sb("his", [P, NG * G + G], I32)
        n_hist = (NG + 1) * G

        loaded, rows_ready, spread, steps, plan_ready, idx_stored = (
            p.sem(n) for n in ("loaded", "rows_ready", "spread", "steps", "plan_ready", "idx_stored"))
        gathered = [p.sem(f"gathered{k}") for k in range(VC)]
        made, stored, turned, taken = (p.sem(n) for n in ("made", "stored", "turned", "taken"))
        block_row_in = p.sem("block_row_in")

        with nc.Block() as block:
            @block.sync
            def _(sp):
                sp.dma_start(ends_i[:], edge["ends"].rearrange("(o k) g -> o k g", o=1)).then_inc(loaded, 16)
                sp.dma_start(vis[:], c["visit_ids"]).then_inc(loaded, 16)
                sp.dma_start(git[:], c["group_ids"][:, 0:NG].broadcast_to([P, NG])).then_inc(loaded, 16)
                sp.dma_start(his[:, 0:n_hist], edge["src"].rearrange("g e -> (g e)").rearrange("(p j) -> p j", p=P)).then_inc(loaded, 16)
                sp.wait_ge(plan_ready, 1)
                with nc.allow_non_contiguous_dma(reason="a few hundred block numbers, once"):
                    sp.dma_start(dram["blocks"].rearrange("(c p) -> p c", c=VC), bvi[:]).then_inc(idx_stored, 16)
                sp.wait_ge(idx_stored, 16)
                sp.dma_start(res["blocks"][:], dram["blocks"].rearrange("(o v) -> o v", o=1)).then_inc(block_row_in, 16)
                for k in range(VC):
                    sp.wait_ge(made, k + 1)
                    sp.dma_start(dram["feat"][k * VP:(k + 1) * VP], feat[:, k % 2]).then_inc(stored, 16)
                    sp.dma_start(dram["flag"][k * VP:(k + 1) * VP], flag[:, k % 2]).then_inc(stored, 16)
                    sp.wait_ge(stored, 32 * (k + 1))
                sp.wait_ge(block_row_in, 16)

            @block.gpsimd
            def _(pool):
                pool.wait_ge(plan_ready, 1)
                for k in range(VC):
                    for out, tab in ((dst_g, "dst"), (src_g, "src"), (et_g, "et")):
                        pool.indirect_dma_start(out[:, k, :], None, edge[tab],
                                                bass.IndirectOffsetOnAxis(ap=tvi[:, k:k + 1], axis=0)).then_inc(gathered[k], 16)

            @block.tensor
            def _(pe):
                pe.wait_ge(rows_ready, 1)
                nc.tensor.matmul(ps_first[:, 0:NG], ones_row[:], ends_f[:, 0, :], start=True, stop=True)
                nc.tensor.matmul(ps_last[:, 0:NG], ones_row[:], ends_f[:, 1, :], start=True, stop=True).then_inc(spread, 1)
                for k in range(VC):
                    pe.wait_ge(made, k + 1)
                    if k:
                        pe.wait_ge(taken, k)
                    for ps, rows in zip(ps_t, (ia, ib, last)):
                        for g in range(G):
                            mm = nc.tensor.transpose(ps[:, g, :], rows[:, k % 2, g * P:(g + 1) * P], c["ident"][0:VP, 0:VP])
                    mm.then_inc(turned, 1)

            @block.vector
            def _(dve):
                link = Chain(dve, steps)
                link(nc.vector.memset(ones_row[:], 1.0))
                link(nc.vector.memset(ones_g[:], 1.0))
                dve.wait_ge(loaded, 64)
                link(nc.vector.tensor_scalar(ends_b[:], ends_i[:], 7, None, ALU.logical_shift_right))
                nc.vector.tensor_copy(ends_f[:], ends_b[:]).then_inc(rows_ready, 1)
                link(nc.vector.tensor_scalar(lo_i[:, 0:n_hist], his[:, 0:n_hist], P - 1, None, ALU.bitwise_and))
                link(nc.vector.tensor_scalar(hi_i[:, 0:n_hist], his[:, 0:n_hist], 7, None, ALU.logical_shift_right))
                link(nc.vector.memset(res["src_lo"][:], -1.0))
                link(nc.vector.memset(res["src_hi"][:], -1.0))
                link(nc.vector.tensor_copy(res["src_lo"][:, 0:n_hist], lo_i[:, 0:n_hist]))
                link(nc.vector.tensor_copy(res["src_hi"][:, 0:n_hist], hi_i[:, 0:n_hist]))
                dve.wait_ge(spread, 1)
                link(nc.vector.tensor_copy(blk_first[:], ps_first[:, 0:NG]))
                link(nc.vector.scalar_tensor_tensor(n_blocks[:], ps_last[:, 0:NG], 1.0, blk_first[:], ALU.add, ALU.subtract))
                link(nc.vector.tensor_tensor_scan(csum[:], ones_g[:], n_blocks[:], 0.0, ALU.mult, ALU.add))
                link(nc.vector.tensor_tensor(base[:], blk_first[:], csum[:], ALU.subtract))
                link(nc.vector.tensor_tensor(base[:], base[:], n_blocks[:], ALU.add))
                for k in range(VC):
                    link(nc.vector.tensor_scalar(junk[0:VP], csum[0:VP], vis[:, k:k + 1], 0.0, ALU.is_le, ALU.add,
                                                 accum_out=tv[:, k:k + 1]))
                    link(nc.vector.scalar_tensor_tensor(junk[0:VP], git[0:VP], tv[:, k:k + 1], base[0:VP],
                                                        ALU.is_equal, ALU.mult, accum_out=bv[:, k:k + 1]))
                link(nc.vector.tensor_tensor(bv[:], bv[:], vis[:], ALU.add))
                link(nc.vector.tensor_scalar(bv[:], bv[:], float(NT - 1), 0.0, ALU.min, ALU.max))
                link(nc.vector.tensor_scalar(shift[:], bv[:], -float(P), None, ALU.mult))
                link(nc.vector.tensor_copy(tvi[:], tv[:]))
                nc.vector.tensor_copy(bvi[:], bv[:]).then_inc(plan_ready, 1)
                dve.wait_ge(plan_ready, 1)

                def take(k):
                    dve.wait_ge(turned, k + 1)
                    vs = slice(k * VP, (k + 1) * VP)
                    for ps, out in zip(ps_t, (res["idx_typed"], res["idx_src"], res["last"])):
                        ins = nc.vector.tensor_copy(out[:, vs, :], ps[:].rearrange("p g v -> p v g"))
                    ins.then_inc(taken, 1)

                for k in range(VC):
                    s = k % 2
                    dve.wait_ge(gathered[k], 48)
                    if k >= 2:
                        dve.wait_ge(stored, 32 * (k - 1))
                    link(nc.vector.tensor_scalar(dl[:], dst_g[:, k, :], shift[:, k:k + 1], -1.0, ALU.add, ALU.max))
                    link(nc.vector.tensor_scalar(dl[:], dl[:], float(P), None, ALU.min))
                    link(nc.vector.tensor_tensor(sq[:], dl[:], dl[:], ALU.mult))
                    link(nc.vector.tensor_scalar(hi[:], sq[:], 7, None, ALU.logical_shift_right))
                    link(nc.vector.tensor_scalar(lo[:], sq[:], P - 1, None, ALU.bitwise_and))
                    link(nc.vector.tensor_copy(feat[:, s, 0, :], hi[:]))
                    link(nc.vector.tensor_copy(feat[:, s, 1, :], lo[:]))
                    link(nc.vector.tensor_copy(feat[:, s, 2, :], dl[:]))
                    link(nc.vector.memset(feat[:, s, 3:5, :], 1.0))
                    link(nc.vector.tensor_tensor(last[:, s, 0:GE - 1], dst_g[:, k, 1:GE], dst_g[:, k, 0:GE - 1], ALU.not_equal))
                    link(nc.vector.tensor_scalar(flag[:, s, 1:GE], last[:, s, 0:GE - 1], -BIG, None, ALU.mult))
                    link(nc.vector.memset(flag[:, s, 0:1], -BIG))
                    link(nc.vector.memset(last[:, s, GE - 1:GE], 1.0))
                    link(nc.vector.tensor_copy(ib[:, s, :], src_g[:, k, :]))
                    link(nc.vector.tensor_scalar(ia[:, s, :], ib[:, s, :], float(R), None, ALU.mult))
                    nc.vector.tensor_tensor(ia[:, s, :], ia[:, s, :], et_g[:, k, :], ALU.add).then_inc(made, 1)
                    take(k)


def edge_pass(nc, name, c, dram, res, table, idx, width, heads, dot, softmax, acc, q=None, hist=None):
    hd = D // heads if heads else D
    hw = hd + 1
    aw = heads * hw if heads else D + 1
    weighted = heads > 0
    RING = 4
    with phase(nc, name) as p:
        rows = p.sb("rows", [P, RING, G, width])
        idx_r = p.sb("idx_r", [P, RING, G], I32)
        feat_r = p.sb("feat_r", [5, RING, GE], BF16)
        flag_r = p.sb("flag_r", [4, RING, GE])
        last_r = p.sb("last_r", [P, RING, G])
        pick = p.sb("pick", [P, RING, GE])
        pick_t = p.sb("pick_t", [P, RING, GE])
        prod = p.sb("prod", [P, GE])
        logit = p.sb("logit", [P, 2, G * max(heads, 1)])
        gap = p.sb("gap", [P, G * max(heads, 1)])
        run = p.sb("run", [4, GE])
        marked = p.sb("marked", [P, G, 5])
        absent = p.sb("absent", [P, 1])
        turns = p.sb("turns", [1, 2])
        top = p.sb("top", [P, 4])
        drop, fade = p.sb("drop", [P, 2, 4]), p.sb("fade", [P, 2, 4])
        wv = p.sb("wv", [P, 2, G, aw])
        lo_hot, hi_hot = p.sb("lo_hot", [P, 2, G, P], BF16), p.sb("hi_hot", [P, 2, G, NT], BF16)

        ps_pick, ps_pick_t = p.ps("ps_pick", [P, GE]), p.ps("ps_pick_t", [P, GE])
        if dot:
            ps_q = [p.ps("ps_q0", [P, GE]), p.ps("ps_q1", [P, GE])]
        else:
            ps_hist = p.ps("ps_hist", [P, 512])
            ps_q = [p.ps("ps_q", [P, 512])] * 2
        ps_turn, ps_back = p.ps("ps_turn", [4, GE]), p.ps("ps_back", [P, 2, 256])
        ps_top, ps_sum = p.ps("ps_top", [P, 512]), p.ps("ps_sum", [P, 512])

        idx_in = [p.sem(f"idx_in{k}") for k in range(RING)]
        feat_in = [p.sem(f"feat_in{k}") for k in range(RING)]
        seg_in = [p.sem(f"seg_in{k}") for k in range(RING)]
        rows_in = [p.sem(f"rows_in{k}") for k in range(RING)]
        (squares, pick_done, pick_t_done, q_done, prod_done, logit_done, turn_done, run_done, back_done, marked_done,
         top_part, absent_done, top_done, drop_done, ref_done, gap_part, gap_done, weight_done, wv_done, fade_done,
         sum_done, faded, acc_done, one, hot_done, hist_done, top_kept, gate) = (p.sem(n) for n in (
            "squares", "pick_done", "pick_t_done", "q_done", "prod_done", "logit_done", "turn_done", "run_done",
            "back_done", "marked_done", "top_part", "absent_done", "top_done", "drop_done", "ref_done", "gap_part",
            "gap_done", "weight_done", "wv_done", "fade_done", "sum_done", "faded", "acc_done", "one", "hot_done",
            "hist_done", "top_kept", "gate"))

        def visits(eng, body, ahead):
            for i in range(-ahead, RING):
                body(i, i % RING, i // RING)
            with eng.Fori(1, NV // RING - 1) as it:
                for k in range(RING):
                    body(it * RING + k, k, it)
            for i in range(NV - RING, NV + 2):
                body(i, i % RING, i // RING)

        def at(i, k, it, d):
            if isinstance(i, int):
                u = i + d
                return (u, u % RING, u // RING) if 0 <= u < NV else None
            return i + d, (k + d) % RING, it + (k + d) // RING

        def block_of(eng, u):
            return eng.value_load(res["blocks"][0:1, bass.ds(u, 1)], min_val=0, max_val=NT - 1)

        wv4 = wv[:].rearrange("p s g (h w) -> p s g h w", w=hw) if weighted else None

        with nc.Block() as block:
            @block.sync
            def _(sp):
                def body(i, k, it):
                    if (v := at(i, k, it, 0)) is None:
                        return
                    u, k, it = v
                    if known(u, RING):
                        sp.wait_ge(rows_in[k], it * 64)
                    sp.dma_start(idx_r[:, k, :], idx[:, bass.ds(u, 1), :].rearrange("p v g -> p (v g)")).then_inc(idx_in[k], 16)
                    if known(u, RING):
                        sp.wait_ge(squares, u - (RING - 1))
                    sp.dma_start(feat_r[:, k, :], dram["feat"][bass.ds(u, 1)].rearrange("v f e -> (v f) e")).then_inc(feat_in[k], 16)
                    if softmax:
                        if known(u, RING):
                            sp.wait_ge(run_done, u - (RING - 1))
                            sp.wait_ge(marked_done, u - (RING - 1))
                        sp.dma_start(flag_r[:, k, :], dram["flag"][bass.ds(u, 1), :].broadcast_to([4, GE])).then_inc(seg_in[k], 16)
                        sp.dma_start(last_r[:, k, :], res["last"][:, bass.ds(u, 1), :].rearrange("p v g -> p (v g)")).then_inc(seg_in[k], 16)
                visits(sp, body, 0)

            @block.gpsimd
            def _(pool):
                nc.gpsimd.memset(turns[:], 0.0).then_inc(one, 1)
                pool.wait_ge(one, 1)

                def body(i, k, it):
                    if (v := at(i, k, it, 0)) is None:
                        return
                    u, k, it = v
                    pool.wait_ge(idx_in[k], it * 16 + 16)
                    if known(u, RING):
                        pool.wait_ge(wv_done if weighted else sum_done, u - (RING - 1))
                    if known(u, 1):
                        pool.wait_ge(gate, u)
                    nc.gpsimd.tensor_tensor(turns[:, 0:1], turns[:, 1:2], turns[:, 1:2], ALU.add).then_inc(gate, 1)
                    for g in range(G):
                        pool.indirect_dma_start(rows[:, k, g, :], None, table,
                                                bass.IndirectOffsetOnAxis(ap=idx_r[:, k, g:g + 1], axis=0)).then_inc(rows_in[k], 16)
                visits(pool, body, 0)

            @block.tensor
            def _(pe):
                if hist is not None:
                    pe.wait_ge(hot_done, 1)
                    nc.tensor.matmul(ps_hist[:, 0:NT], lo_hot[:, 0, 0, :], hi_hot[:, 0, 0, :], start=True, stop=False,
                                     skip_group_check=True).then_inc(hist_done, 1)

                def body(i, k, it):
                    if v := at(i, k, it, -2):
                        u, s, t = v
                        if weighted:
                            pe.wait_ge(wv_done, u + 1)
                        else:
                            pe.wait_ge(rows_in[s], t * 64 + 64)
                            pe.wait_ge(pick_done, u + 1)
                        if known(u, 1):
                            pe.wait_ge(acc_done, u)
                        for g in range(G):
                            rhs = wv[:, s % 2, g, :] if weighted else rows[:, s, g, :]
                            mm = nc.tensor.matmul(ps_sum[:, 0:aw], pick[:, s, g * P:(g + 1) * P], rhs,
                                                  start=g == 0, stop=g == G - 1)
                        mm.then_inc(sum_done, 1)
                    if v := at(i, k, it, 1):
                        u, s, t = v
                        pe.wait_ge(feat_in[s], t * 16 + 16)
                        if known(u, 1):
                            if weighted:
                                pe.wait_ge(pick_t_done, u)
                            pe.wait_ge(pick_done, u)
                        if weighted:
                            nc.tensor.matmul(ps_pick_t[:], c["col_feat"], feat_r[:, s, :], start=True, stop=True)
                        for g in range(G):
                            mm = nc.tensor.matmul(ps_pick[:, g * P:(g + 1) * P], feat_r[:, s, g * P:(g + 1) * P],
                                                  c["col_feat"], start=True, stop=True)
                        mm.then_inc(squares, 1)
                    if softmax and (v := at(i, k, it, -1)):
                        u, s, t = v
                        pe.wait_ge(run_done, u + 1)
                        if known(u, 1):
                            pe.wait_ge(marked_done, u)
                        for g in range(G):
                            mm = nc.tensor.matmul(ps_back[:, 0, g * 4:(g + 1) * 4], run[:, g * P:(g + 1) * P], c["ident"][0:4, 0:4],
                                                  start=True, stop=True)
                        mm.then_inc(back_done, 1)
                        pe.wait_ge(marked_done, u + 1)
                        if known(u, 1):
                            pe.wait_ge(top_done, u)
                        for g in range(G):
                            mm = nc.tensor.matmul(ps_top[:, 0:5], pick[:, s, g * P:(g + 1) * P], marked[:, g, :],
                                                  start=g == 0, stop=g == G - 1)
                        mm.then_inc(top_part, 1)
                        pe.wait_ge(top_done, u + 1)
                        if known(u, 1):
                            pe.wait_ge(gap_part, u)
                        for g in range(G):
                            mm = nc.tensor.matmul(ps_back[:, 1, g * 4:(g + 1) * 4], pick_t[:, s, g * P:(g + 1) * P], top[:],
                                                  start=True, stop=True)
                        mm.then_inc(ref_done, 1)
                    if hist is not None and (v := at(i, k, it, -1)):
                        u, s, t = v
                        pe.wait_ge(hot_done, u + 2)
                        for g in range(G):
                            mm = nc.tensor.matmul(ps_hist[:, 0:NT], lo_hot[:, s % 2, g, :], hi_hot[:, s % 2, g, :],
                                                  start=False, stop=False, skip_group_check=True)
                        mm.then_inc(hist_done, 1)
                    if softmax and (v := at(i, k, it, 0)):
                        u, s, t = v
                        pe.wait_ge(logit_done, u + 1)
                        if known(u, 1):
                            pe.wait_ge(run_done, u)
                        for g in range(G):
                            mm = nc.tensor.transpose(ps_turn[:, g * P:(g + 1) * P], logit[:, s % 2, g * 4:(g + 1) * 4], c["ident"])
                        mm.then_inc(turn_done, 1)
                    if weighted and (v := at(i, k, it, 1)):
                        u, s, t = v
                        b = block_of(pe, u)
                        qw = D if dot else 4
                        pe.wait_ge(pick_t_done, u + 1)
                        if known(u, len(set(map(id, ps_q)))):
                            pe.wait_ge(prod_done, u + 1 - len(set(map(id, ps_q))))
                        for g in range(G):
                            mm = nc.tensor.matmul(ps_q[s % 2][:, g * qw:(g + 1) * qw], pick_t[:, s, g * P:(g + 1) * P],
                                                  q[:, bass.ds(b * qw, qw)], start=True, stop=True)
                        mm.then_inc(q_done, 1)
                visits(pe, body, 1)

            @block.scalar
            def _(act):
                def body(i, k, it):
                    if v := at(i, k, it, 1):
                        u, s, t = v
                        act.wait_ge(squares, u + 1)
                        if known(u, RING):
                            act.wait_ge(sum_done, u - (RING - 1))
                        if weighted:
                            nc.scalar.activation(pick_t[:, s, :], ps_pick_t[:], ACT.Relu, bias=1.0, scale=-1.0).then_inc(pick_t_done, 1)
                        nc.scalar.activation(pick[:, s, :], ps_pick[:], ACT.Relu, bias=1.0, scale=-1.0).then_inc(pick_done, 1)
                    if weighted and (v := at(i, k, it, -1)):
                        u, s, t = v
                        if softmax:
                            act.wait_ge(drop_done, u + 1)
                            if known(u, 2):
                                act.wait_ge(acc_done, u - 1)
                            nc.scalar.activation(fade[:, s % 2, :], drop[:, s % 2, :], ACT.Exp).then_inc(fade_done, 1)
                        act.wait_ge(gap_done, u + 1)
                        if known(u, 2):
                            act.wait_ge(sum_done, u - 1)
                        nc.scalar.activation(wv4[:, s % 2, :, :, hd], gap[:].rearrange("p (g h) -> p g h", g=G), ACT.Exp).then_inc(weight_done, 1)
                visits(act, body, 1)

            @block.vector
            def _(dve):
                if hist is not None:
                    nc.vector.memset(lo_hot[:, 0, 0, :], 0.0)
                    nc.vector.memset(hi_hot[:, 0, 0, :], 0.0).then_inc(hot_done, 1)

                def running_max(v):
                    u, s, t = v
                    dve.wait_ge(seg_in[s], t * 32 + 32)
                    dve.wait_ge(turn_done, u + 1)
                    nc.vector.tensor_tensor_scan(run[:], flag_r[:, s, :], ps_turn[:], -BIG, ALU.add, ALU.max).then_inc(run_done, 1)

                def mark_last(v):
                    u, s, t = v
                    dve.wait_ge(back_done, u + 1)
                    nc.vector.tensor_tensor(marked[:, :, 0:4], ps_back[:, 0, 0:4 * G].rearrange("p (g h) -> p g h", g=G),
                                            bcast(last_r[:, s, :], [P, G, 4]), ALU.mult)
                    nc.vector.tensor_copy(marked[:, :, 4], last_r[:, s, :]).then_inc(marked_done, 1)

                def logits_a(v):
                    u, s, t = v
                    dve.wait_ge(rows_in[s], t * 64 + 64)
                    dve.wait_ge(q_done, u + 1)
                    if known(u, 1):
                        dve.wait_ge(logit_done, u)
                    if dot:
                        nc.vector.tensor_tensor(prod[:].rearrange("p (g d) -> p g d", g=G), rows[:, s, :, 0:D],
                                                ps_q[s % 2][:].rearrange("p (g d) -> p g d", g=G), ALU.mult).then_inc(prod_done, 1)
                    else:
                        nc.vector.tensor_tensor(prod[:, 0:4 * G].rearrange("p (g h) -> p g h", g=G),
                                                rows[:, s].rearrange("p g (h w) -> p g h w", w=hw)[:, :, :, hd],
                                                ps_q[0][:, 0:4 * G].rearrange("p (g h) -> p g h", g=G), ALU.add).then_inc(prod_done, 1)

                def logits_b(v):
                    u, s, t = v
                    dve.wait_ge(prod_done, u + 1)
                    if dot:
                        nc.vector.reduce_sum(logit[:, s % 2, :], prod[:].rearrange("p (k d) -> p k d", d=hd), AX.X).then_inc(logit_done, 1)
                    else:
                        nc.vector.scalar_tensor_tensor(logit[:, s % 2, :], prod[:, 0:4 * G], SLOPE, prod[:, 0:4 * G],
                                                       ALU.mult, ALU.max).then_inc(logit_done, 1)

                def raise_max(v):
                    u, s, t = v
                    b = block_of(dve, u)
                    kept = res["top"][:, bass.ds(b * 4, 4)]
                    dve.wait_ge(top_part, u + 1)
                    nc.vector.tensor_scalar(absent[:], ps_top[:, 4:5], BIG, -BIG, ALU.mult, ALU.add).then_inc(absent_done, 1)
                    dve.wait_ge(absent_done, u + 1)
                    if known(u, 1):
                        dve.wait_ge(top_kept, u)
                    nc.vector.scalar_tensor_tensor(top[:], ps_top[:, 0:4], absent[:, 0:1], kept, ALU.add, ALU.max).then_inc(top_done, 1)
                    dve.wait_ge(top_done, u + 1)
                    nc.vector.tensor_tensor(drop[:, s % 2, :], kept, top[:], ALU.subtract).then_inc(drop_done, 1)
                    dve.wait_ge(drop_done, u + 1)
                    nc.vector.tensor_scalar(kept, top[:], 1.0, None, ALU.mult).then_inc(top_kept, 1)

                def gaps(v):
                    u, s, t = v
                    if softmax:
                        dve.wait_ge(ref_done, u + 1)
                        nc.vector.tensor_tensor(gap[:], logit[:, s % 2, :], ps_back[:, 1, 0:4 * G], ALU.subtract).then_inc(gap_part, 1)
                        dve.wait_ge(gap_part, u + 1)
                        nc.vector.tensor_scalar(gap[:], gap[:], 0.0, None, ALU.min).then_inc(gap_done, 1)
                    else:
                        dve.wait_ge(logit_done, u + 1)
                        nc.vector.tensor_scalar(gap[:], logit[:, s % 2, :], -5.0, 5.0, ALU.max, ALU.min).then_inc(gap_done, 1)

                def add_sums(v):
                    u, s, t = v
                    b = block_of(dve, u)
                    blk = acc[:, bass.ds(b * aw, aw)]
                    if softmax:
                        dve.wait_ge(fade_done, u + 1)
                        if known(u, 1):
                            dve.wait_ge(acc_done, u)
                        nc.vector.tensor_tensor(blk.rearrange("p (h w) -> p h w", w=hw), blk.rearrange("p (h w) -> p h w", w=hw),
                                                bcast(fade[:, s % 2, :], [P, heads, hw]), ALU.mult).then_inc(faded, 1)
                        dve.wait_ge(faded, u + 1)
                    elif known(u, 1):
                        dve.wait_ge(acc_done, u)
                    dve.wait_ge(sum_done, u + 1)
                    nc.vector.tensor_tensor(blk, blk, ps_sum[:, 0:aw], ALU.add).then_inc(acc_done, 1)

                def weigh(v):
                    u, s, t = v
                    dve.wait_ge(weight_done, u + 1)
                    w = s % 2
                    vals = (rows[:, s, :, D:2 * D].rearrange("p g (h d) -> p g h d", d=hd) if dot
                            else rows[:, s].rearrange("p g (h w) -> p g h w", w=hw)[:, :, :, 0:hd])
                    nc.vector.tensor_tensor(wv4[:, w, :, :, 0:hd], vals, bcast(wv4[:, w, :, :, hd], [P, G, heads, hd]),
                                            ALU.mult).then_inc(wv_done, 1)

                def digits(v):
                    u, s, t = v
                    if known(u, 2):
                        dve.wait_ge(hist_done, u)
                    elif u == 0:
                        dve.wait_ge(hist_done, 1)
                    for g in range(G):
                        nc.vector.tensor_scalar(lo_hot[:, s % 2, g, :], c["iota_bf"][:, 0:P], res["src_lo"][:, bass.ds(u * G + g, 1)],
                                                None, ALU.is_equal)
                        ins = nc.vector.tensor_scalar(hi_hot[:, s % 2, g, :], c["iota_bf"][:, 0:NT],
                                                      res["src_hi"][:, bass.ds(u * G + g, 1)], None, ALU.is_equal)
                    ins.then_inc(hot_done, 1)

                def body(i, k, it):
                    now, before, earlier = at(i, k, it, 0), at(i, k, it, -1), at(i, k, it, -2)
                    if softmax and before:
                        running_max(before)
                    if hist is not None and now:
                        digits(now)
                    if softmax and before:
                        mark_last(before)
                    if weighted and now:
                        logits_a(now)
                    if softmax and before:
                        raise_max(before)
                    if weighted and now:
                        logits_b(now)
                    if weighted and before:
                        gaps(before)
                    if earlier:
                        add_sums(earlier)
                    if weighted and before:
                        weigh(before)
                visits(dve, body, 0)
                if hist is not None:
                    dve.wait_ge(hist_done, NV + 1)
                    nc.vector.tensor_copy(hist, ps_hist[:, 0:NT]).then_inc(one, 1)


class TurnedRows:

    def __init__(self, p, nc, c, x, typed=None, tag=""):
        self.nc, self.c, self.x, self.typed = nc, c, x, typed
        self.n = T if typed is not None else 1
        self.staged_rows = p.sb(tag + "staged_rows", [P, 2, self.n, D])
        self.rows = p.sb(tag + "turned_rows", [P, 2, self.n, P])
        self.ps = p.ps(tag + "ps_turned", [P, self.n, P])
        self.staged, self.turned, self.copied, self.made = (
            p.sem(tag + n) for n in ("staged", "turned", "copied", "made"))

    def stage(self, pool, t, s):
        if known(t, 2):
            pool.wait_ge(self.turned, t - 1)
        tile = self.x[:, bass.ds(t, 1), :]
        if self.typed is None:
            self.nc.gpsimd.tensor_copy(self.staged_rows[:, s], tile).then_inc(self.staged, 1)
        else:
            shape = [P, T, D]
            kinds = self.typed[:, bass.ds(t, 1), :].rearrange("p t y -> p (t y)")
            self.nc.gpsimd.tensor_tensor(self.staged_rows[:, s], tile.broadcast_to(shape), bcast(kinds, shape),
                                         ALU.mult).then_inc(self.staged, 1)

    def turn(self, pe, t, s):
        pe.wait_ge(self.staged, t + 1)
        if known(t, 1):
            pe.wait_ge(self.copied, t)
        for y in range(self.n):
            mm = self.nc.tensor.transpose(self.ps[:, y, :], self.staged_rows[:, s, y, :], self.c["ident"])
        mm.then_inc(self.turned, 1)

    def copy(self, act, t, s):
        act.wait_ge(self.turned, t + 1)
        if known(t, 2):
            act.wait_ge(self.made, t - 1)
        self.nc.scalar.activation(self.rows[:, s], self.ps[:], ACT.Copy).then_inc(self.copied, 1)


def norm_phase(nc, name, x, out, square, **how):
    with phase(nc, name) as p:
        ln = LayerNorm(p, x, out, square, **how)
        with nc.Block() as block:
            @block.vector
            def _(dve):
                ln.vector(nc, dve)

            @block.scalar
            def _(act):
                ln.scalar(nc, act)


def tile(x, t):
    return x[:, bass.ds(t, 1), :].rearrange("p t d -> p (t d)")


def row_of(ap):
    return ap.rearrange("(o d) -> o d", o=1).broadcast_to([P, ap.shape[0]])


def typed_tables(nc, c, w, h, typed, q, dram):
    with phase(nc, "l0pre") as p:
        wkv, wqp = p.sb("wkv", [P, T, 2, D]), p.sb("wqp", [P, T, 2, D])
        rel = p.sb("rel", [P, 2, R, D])
        pri = p.sb("pri", [P, 4, R])
        kv_t = p.sb("kv_t", [P, 2, 2, P])
        pre = p.sb("pre", [P, 2, D])
        out = p.sb("out", [P, 2, R, 2, D])
        tr = TurnedRows(p, nc, c, h, typed)
        ps_kv, ps_qp = p.ps("ps_kv", [P, 2, 256]), p.ps("ps_qp", [P, 2, 256])
        ps_rel = [p.ps(f"ps_rel{j}", [P, 4, D]) for j in range(4)]
        loaded, zeroed, scaled, rel_in, steps, kv_made, kv_copied, rel_made, rel_k, rel_v, q_taken, pre_taken = (
            p.sem(n) for n in ("loaded", "zeroed", "scaled", "rel_in", "steps", "kv_made", "kv_copied", "rel_made",
                               "rel_k", "rel_v", "q_taken", "pre_taken"))
        stored = [p.sem("stored0"), p.sem("stored1")]

        with nc.Block() as block:
            @block.sync
            def _(sp):
                for i, name in enumerate(("L0_gnn_W_k", "L0_gnn_W_v")):
                    sp.dma_start(wkv[:, :, i, :], w[name].rearrange("t i o -> i t o")).then_inc(loaded, 16)
                for i, name in enumerate(("L0_gnn_W_q", "L0_gnn_W_pre")):
                    sp.dma_start(wqp[:, :, i, :], w[name].rearrange("t i o -> i t o")).then_inc(loaded, 16)
                sp.dma_start(pri[:].rearrange("p h r -> p (h r)"), row_of(w["L0_gnn_rel_pri"].rearrange("h r -> (h r)"))).then_inc(loaded, 16)
                sp.wait_ge(zeroed, 1)
                for hh in range(4):
                    for i, name in enumerate(("L0_gnn_rel_att", "L0_gnn_rel_msg")):
                        sp.dma_start(rel[32 * hh:32 * hh + 32, i, :, 32 * hh:32 * hh + 32],
                                     w[name][hh].rearrange("r d f -> d r f")).then_inc(rel_in, 16)

                def store(t, s, turn):
                    sp.wait_ge(rel_k, t + 1)
                    sp.wait_ge(rel_v, t + 1)
                    sp.dma_start(dram["kv_typed"][bass.ds(t, 1)].rearrange("t p f -> (t p) f"),
                                 out[:, s].rearrange("p r k d -> p (r k d)")).then_inc(stored[s], 16)
                    sp.wait_ge(pre_taken, t + 1)
                    sp.dma_start(tile(dram["pre"], t), pre[:, s]).then_inc(stored[s], 16)
                node_tiles(sp, store)
                sp.wait_ge(stored[0], 32 * (NT // 2 + 1))
                sp.wait_ge(stored[1], 32 * (NT // 2))

            @block.gpsimd
            def _(pool):
                node_tiles(pool, lambda t, s, turn: tr.stage(pool, t, s))

            @block.tensor
            def _(pe):
                pe.wait_ge(loaded, 80)
                pe.wait_ge(scaled, 1)

                def body(t, s, turn):
                    tr.turn(pe, t, s)
                    pe.wait_ge(tr.copied, t + 1)
                    if known(t, 1):
                        pe.wait_ge(kv_copied, t)
                        pe.wait_ge(q_taken, t)
                        pe.wait_ge(pre_taken, t)
                    for i in range(2):
                        for y in range(T):
                            mm = nc.tensor.matmul(ps_kv[:, i, 0:P], wkv[:, y, i, :], tr.rows[:, s, y, :], start=y == 0, stop=y == T - 1)
                    mm.then_inc(kv_made, 1)
                    for y in range(T):
                        mm = nc.tensor.matmul(ps_qp[:, 0, :], tr.rows[:, s, y, :], wqp[:, y, :, :], start=y == 0, stop=y == T - 1)
                    mm.then_inc(tr.made, 1)
                    pe.wait_ge(kv_copied, t + 1)
                    if known(t, 1):
                        pe.wait_ge(rel_k, t)
                        pe.wait_ge(rel_v, t)
                    for i in range(2):
                        for half in range(2):
                            mm = nc.tensor.matmul(ps_rel[2 * i + half][:], kv_t[:, s, i, :], rel[:, i, 4 * half:4 * half + 4, :],
                                                  start=True, stop=True)
                    mm.then_inc(rel_made, 1)
                node_tiles(pe, body)

            @block.scalar
            def _(act):
                def body(t, s, turn):
                    tr.copy(act, t, s)
                    act.wait_ge(kv_made, t + 1)
                    if known(t, 2):
                        act.wait_ge(rel_made, t - 1)
                    nc.scalar.activation(kv_t[:, s], ps_kv[:, :, 0:P], ACT.Copy).then_inc(kv_copied, 1)
                    act.wait_ge(tr.made, t + 1)
                    if known(t, 2):
                        act.wait_ge(stored[s], turn * 32)
                    nc.scalar.activation(pre[:, s], ps_qp[:, 0, D:2 * D], ACT.Copy).then_inc(pre_taken, 1)
                    nc.scalar.activation(tile(q, t), ps_qp[:, 0, 0:D], ACT.Copy).then_inc(q_taken, 1)
                    act.wait_ge(rel_made, t + 1)
                    for half in range(2):
                        ins = nc.scalar.activation(out[:, s, 4 * half:4 * half + 4, 1, :], ps_rel[2 + half][:], ACT.Copy)
                    ins.then_inc(rel_v, 1)
                node_tiles(act, body)

            @block.vector
            def _(dve):
                link = Chain(dve, steps)
                nc.vector.memset(rel[:], 0.0).then_inc(zeroed, 1)
                dve.wait_ge(loaded, 80)
                link(nc.vector.tensor_scalar(pri[:], pri[:], float(1.0 / np.sqrt(32.0)), None, ALU.mult))
                dve.wait_ge(rel_in, 128)
                for r in range(R):
                    block_r = rel[:, 0, r, :].rearrange("p (h f) -> p h f", f=32)
                    ins = nc.vector.tensor_tensor(block_r, block_r, bcast(pri[:, :, r], [P, 4, 32]), ALU.mult)
                ins.then_inc(scaled, 1)

                def body(t, s, turn):
                    dve.wait_ge(rel_made, t + 1)
                    if known(t, 2):
                        dve.wait_ge(stored[s], turn * 32)
                    for half in range(2):
                        ins = nc.vector.tensor_copy(out[:, s, 4 * half:4 * half + 4, 0, :], ps_rel[half][:])
                    ins.then_inc(rel_k, 1)
                node_tiles(dve, body)


def typed_output(nc, c, w, x, h, typed, acc, mix, dram):
    with phase(nc, "l0post") as p:
        wa = p.sb("wa", [P, T, D])
        skip = p.sb("skip", [P, T])
        alpha, rest = p.sb("alpha", [P, NT]), p.sb("rest", [P, NT])
        picked = p.sb("picked", [P, NT, T])
        tr = TurnedRows(p, nc, c, mix, typed)
        ps_out = p.ps("ps_out", [P, 2, 512])
        loaded, steps, negated, gated, mixed, done = (p.sem(n) for n in ("loaded", "steps", "negated", "gated", "mixed", "done"))
        acc4 = acc.rearrange("p (t h w) -> p t h w", h=4, w=33)
        with nc.Block() as block:
            @block.sync
            def _(sp):
                sp.dma_start(wa[:], w["L0_gnn_W_a"].rearrange("t i o -> i t o")).then_inc(loaded, 16)
                sp.dma_start(skip[:], row_of(w["L0_gnn_skip"])).then_inc(loaded, 16)
                sp.dma_start(mix, dram["pre"]).then_inc(loaded, 16)

            @block.scalar
            def _(act):
                act.wait_ge(negated, 1)
                nc.scalar.activation(skip[:], skip[:], ACT.Exp, scale=-1.0).then_inc(gated, 1)
                node_tiles(act, lambda t, s, turn: tr.copy(act, t, s))

            @block.gpsimd
            def _(pool):
                pool.wait_ge(mixed, 1)
                node_tiles(pool, lambda t, s, turn: tr.stage(pool, t, s))

            @block.tensor
            def _(pe):
                def body(t, s, turn):
                    tr.turn(pe, t, s)
                    pe.wait_ge(tr.copied, t + 1)
                    if known(t, 2):
                        pe.wait_ge(done, t - 1)
                    for y in range(T):
                        mm = nc.tensor.matmul(ps_out[:, s, 0:D], tr.rows[:, s, y, :], wa[:, y, :], start=y == 0, stop=y == T - 1)
                    mm.then_inc(tr.made, 1)
                node_tiles(pe, body)

            @block.vector
            def _(dve):
                link = Chain(dve, steps)
                z = acc4[:, :, :, 32]
                link(nc.vector.tensor_scalar(z, z, 1e-30, None, ALU.max))
                link(nc.vector.reciprocal(z, z))
                dve.wait_ge(loaded, 48)
                nc.vector.tensor_copy(picked[:], typed).then_inc(negated, 1)
                link(nc.vector.tensor_tensor(acc4[:, :, :, 0:32], acc4[:, :, :, 0:32], bcast(z, [P, NT, 4, 32]), ALU.mult))
                link(nc.vector.tensor_scalar(mix, mix, 1.0 - LAM, None, ALU.mult))
                link(nc.vector.tensor_scalar(acc4[:, :, :, 0:32], acc4[:, :, :, 0:32], LAM, None, ALU.mult))
                nc.vector.tensor_tensor(mix.rearrange("p t (h f) -> p t h f", f=32), mix.rearrange("p t (h f) -> p t h f", f=32),
                                        acc4[:, :, :, 0:32], ALU.add).then_inc(mixed, 1)
                dve.wait_ge(gated, 1)
                link(nc.vector.tensor_scalar(skip[:], skip[:], 1.0, None, ALU.add))
                link(nc.vector.reciprocal(skip[:], skip[:]))
                link(nc.vector.tensor_tensor(picked[:], typed, skip[:].unsqueeze(1).broadcast_to([P, NT, T]), ALU.mult))
                link(nc.vector.reduce_sum(alpha[:], picked[:], AX.X))
                link(nc.vector.tensor_scalar(rest[:], alpha[:], -1.0, 1.0, ALU.mult, ALU.add))
                link(nc.vector.tensor_tensor(h, h, bcast(rest[:], [P, NT, D]), ALU.mult))
                link(nc.vector.tensor_tensor(x, x, h, ALU.add))

                def body(t, s, turn):
                    dve.wait_ge(tr.made, t + 1)
                    nc.vector.scalar_tensor_tensor(tile(x, t), ps_out[:, s, 0:D], alpha[:, bass.ds(t, 1)], tile(x, t),
                                                   ALU.mult, ALU.add).then_inc(done, 1)
                node_tiles(dve, body)


def gat_tables(nc, c, w, g, acc, top, ad, dram):
    with phase(nc, "l1pre") as p:
        wt = p.sb("wt", [P, D])
        att = p.sb("att", [P, 2, D])
        part = p.sb("part", [P, NT, D])
        tr = TurnedRows(p, nc, c, g)
        ps_out = p.ps("ps_out", [P, 2, 512])
        loaded, steps, done, table_ready, table_out = (p.sem(n) for n in ("loaded", "steps", "done", "table_ready", "table_out"))
        acc4 = acc.rearrange("p (t h w) -> p t h w", h=4, w=33)
        with nc.Block() as block:
            @block.sync
            def _(sp):
                sp.dma_start(wt[:], w["L1_gnn_W"]).then_inc(loaded, 16)
                sp.dma_start(att[:, 0, :], row_of(w["L1_gnn_att_src"].rearrange("h c -> (h c)"))).then_inc(loaded, 16)
                sp.dma_start(att[:, 1, :], row_of(w["L1_gnn_att_dst"].rearrange("h c -> (h c)"))).then_inc(loaded, 16)
                sp.wait_ge(table_ready, 1)
                sp.dma_start(dram["gat"].rearrange("(t p) f -> p t f", p=P), acc.rearrange("p (t f) -> p t f", t=NT)).then_inc(table_out, 16)
                sp.wait_ge(table_out, 16)

            @block.scalar
            def _(act):
                node_tiles(act, lambda t, s, turn: tr.copy(act, t, s))

            @block.gpsimd
            def _(pool):
                node_tiles(pool, lambda t, s, turn: tr.stage(pool, t, s))

            @block.tensor
            def _(pe):
                pe.wait_ge(loaded, 48)

                def body(t, s, turn):
                    tr.turn(pe, t, s)
                    pe.wait_ge(tr.copied, t + 1)
                    if known(t, 2):
                        pe.wait_ge(done, t - 1)
                    nc.tensor.matmul(ps_out[:, s, 0:D], tr.rows[:, s, 0, :], wt[:], start=True, stop=True).then_inc(tr.made, 1)
                node_tiles(pe, body)

            @block.vector
            def _(dve):
                link = Chain(dve, steps)

                def body(t, s, turn):
                    dve.wait_ge(tr.made, t + 1)
                    nc.vector.tensor_scalar(acc[:, bass.ds(t * 132, 132)].rearrange("p (h w) -> p h w", w=33)[:, :, 0:32],
                                            ps_out[:, s, 0:D].rearrange("p (h f) -> p h f", f=32), 1.0, None, ALU.mult).then_inc(done, 1)
                node_tiles(dve, body)
                dve.wait_ge(done, NT)
                dve.wait_ge(loaded, 48)
                rows4 = part[:].rearrange("p t (h f) -> p t h f", f=32)
                for i, out in ((0, acc4[:, :, :, 32]), (1, ad.rearrange("p (t h) -> p t h", h=4))):
                    for hh in range(4):
                        ins = nc.vector.tensor_tensor(rows4[:, :, hh, :], acc4[:, :, hh, 0:32],
                                                      att[:, i, 32 * hh:32 * hh + 32].unsqueeze(1).broadcast_to([P, NT, 32]), ALU.mult)
                    link(ins)
                    link(nc.vector.reduce_sum(out, rows4, AX.X))
                top3 = top.rearrange("p (t h) -> p t h", h=4)
                link(nc.vector.tensor_tensor(top3, acc4[:, :, :, 32], ad.rearrange("p (t h) -> p t h", h=4), ALU.add))
                nc.vector.scalar_tensor_tensor(top, top, SLOPE, top, ALU.mult, ALU.max).then_inc(table_ready, 1)
                dve.wait_ge(table_out, 16)
                link(nc.vector.memset(acc4[:, :, :, 32], 1.0))


def gat_output(nc, c, w, h, acc, g):
    with phase(nc, "l1post") as p:
        bias = p.sb("bias", [P, D])
        loaded, steps = p.sem("loaded"), p.sem("steps")
        acc4 = acc.rearrange("p (t h w) -> p t h w", h=4, w=33)
        with nc.Block() as block:
            @block.sync
            def _(sp):
                sp.dma_start(bias[:], row_of(w["L1_gnn_gat_b"])).then_inc(loaded, 16)

            @block.vector
            def _(dve):
                link = Chain(dve, steps)
                z = acc4[:, :, :, 32]
                link(nc.vector.reciprocal(z, z))
                link(nc.vector.tensor_tensor(g.rearrange("p t (h f) -> p t h f", f=32), acc4[:, :, :, 0:32], bcast(z, [P, NT, 4, 32]), ALU.mult))
                dve.wait_ge(loaded, 16)
                link(nc.vector.tensor_tensor(g, g, bias[:].unsqueeze(1).broadcast_to([P, NT, D]), ALU.add))
                link(nc.vector.tensor_tensor(g, g, h, ALU.add))


def feed_forward(nc, name, c, w1, b1, w2, b2, func, x, into):
    with phase(nc, name) as p:
        w1s, w2s = p.sb("w1s", [P, 2 * D]), p.sb("w2s", [P, 2, D])
        b1s, b2s = p.sb("b1s", [P, 2]), p.sb("b2s", [P, D])
        hidden = p.sb("hidden", [P, 2, 2, P])
        tr = TurnedRows(p, nc, c, x)
        ps_hid, ps_out = p.ps("ps_hid", [P, 2, 256]), p.ps("ps_out", [P, 2, 512])
        loaded, hid_done, out_made, done, biased = (p.sem(n) for n in ("loaded", "hid_done", "out_made", "done", "biased"))
        with nc.Block() as block:
            @block.sync
            def _(sp):
                sp.dma_start(w1s[:], w1).then_inc(loaded, 16)
                sp.dma_start(w2s[:], w2.rearrange("(c k) o -> k c o", c=2)).then_inc(loaded, 16)
                sp.dma_start(b1s[:], b1).then_inc(loaded, 16)
                sp.dma_start(b2s[:], row_of(b2)).then_inc(loaded, 16)

            @block.gpsimd
            def _(pool):
                node_tiles(pool, lambda t, s, turn: tr.stage(pool, t, s))

            @block.tensor
            def _(pe):
                pe.wait_ge(loaded, 64)

                def body(t, s, turn):
                    tr.turn(pe, t, s)
                    pe.wait_ge(tr.copied, t + 1)
                    if known(t, 1):
                        pe.wait_ge(hid_done, t)
                    for j in range(2):
                        mm = nc.tensor.matmul(ps_hid[:, j, 0:P], w1s[:, j * D:(j + 1) * D], tr.rows[:, s, 0, :], start=True, stop=True)
                    mm.then_inc(tr.made, 1)
                    pe.wait_ge(hid_done, t + 1)
                    if known(t, 2):
                        pe.wait_ge(done, t - 1)
                    for j in range(2):
                        mm = nc.tensor.matmul(ps_out[:, s, 0:D], hidden[:, s, j, :], w2s[:, j, :], start=j == 0, stop=j == 1)
                    mm.then_inc(out_made, 1)
                node_tiles(pe, body)

            @block.scalar
            def _(act):
                act.wait_ge(loaded, 64)

                def body(t, s, turn):
                    tr.copy(act, t, s)
                    act.wait_ge(tr.made, t + 1)
                    if known(t, 2):
                        act.wait_ge(out_made, t - 1)
                    for j in range(2):
                        ins = nc.scalar.activation(hidden[:, s, j, :], ps_hid[:, j, 0:P], func, bias=b1s[:, j:j + 1])
                    ins.then_inc(hid_done, 1)
                node_tiles(act, body)

            @block.vector
            def _(dve):
                dve.wait_ge(loaded, 64)
                nc.vector.tensor_tensor(into, into, b2s[:].unsqueeze(1).broadcast_to([P, NT, D]), ALU.add).then_inc(biased, 1)
                dve.wait_ge(biased, 1)

                def body(t, s, turn):
                    dve.wait_ge(out_made, t + 1)
                    nc.vector.tensor_tensor(tile(into, t), tile(into, t), ps_out[:, s, 0:D], ALU.add).then_inc(done, 1)
                node_tiles(dve, body)


def conv_table(nc, h, out_deg, part, dram):
    with phase(nc, "l2pre") as p:
        steps, clipped, rooted, ready, stored = (p.sem(n) for n in ("steps", "clipped", "rooted", "ready", "stored"))
        with nc.Block() as block:
            @block.scalar
            def _(act):
                act.wait_ge(clipped, 1)
                nc.scalar.activation(out_deg, out_deg, ACT.Sqrt).then_inc(rooted, 1)

            @block.vector
            def _(dve):
                link = Chain(dve, steps)
                nc.vector.tensor_scalar(out_deg, out_deg, 1.0, None, ALU.max).then_inc(clipped, 1)
                dve.wait_ge(rooted, 1)
                link(nc.vector.reciprocal(out_deg, out_deg))
                nc.vector.memset(part[:, :, D:D + 1], 1.0)
                nc.vector.tensor_tensor(part[:, :, 0:D], h, bcast(out_deg, [P, NT, D]), ALU.mult).then_inc(ready, 1)

            @block.sync
            def _(sp):
                sp.wait_ge(ready, 1)
                sp.dma_start(dram["conv"].rearrange("(t p) f -> p t f", p=P), part).then_inc(stored, 16)
                sp.wait_ge(stored, 16)


def conv_output(nc, c, w, x, acc, g):
    with phase(nc, "l2post") as p:
        wt, bias, deg = p.sb("wt", [P, D]), p.sb("bias", [P, D]), p.sb("deg", [P, NT])
        tr = TurnedRows(p, nc, c, acc[:, :, 0:D])
        ps_out = p.ps("ps_out", [P, 2, 512])
        loaded, steps, clipped, rooted, done = (p.sem(n) for n in ("loaded", "steps", "clipped", "rooted", "done"))
        with nc.Block() as block:
            @block.sync
            def _(sp):
                sp.dma_start(wt[:], w["L2_gnn_weight"]).then_inc(loaded, 16)
                sp.dma_start(bias[:], row_of(w["L2_gnn_bias"])).then_inc(loaded, 16)

            @block.scalar
            def _(act):
                act.wait_ge(clipped, 1)
                nc.scalar.activation(deg[:], deg[:], ACT.Sqrt).then_inc(rooted, 1)
                node_tiles(act, lambda t, s, turn: tr.copy(act, t, s))

            @block.gpsimd
            def _(pool):
                node_tiles(pool, lambda t, s, turn: tr.stage(pool, t, s))

            @block.tensor
            def _(pe):
                pe.wait_ge(loaded, 32)

                def body(t, s, turn):
                    tr.turn(pe, t, s)
                    pe.wait_ge(tr.copied, t + 1)
                    if known(t, 2):
                        pe.wait_ge(done, t - 1)
                    nc.tensor.matmul(ps_out[:, s, 0:D], tr.rows[:, s, 0, :], wt[:], start=True, stop=True).then_inc(tr.made, 1)
                node_tiles(pe, body)

            @block.vector
            def _(dve):
                link = Chain(dve, steps)
                nc.vector.tensor_scalar(deg[:], acc[:, :, D], 1.0, None, ALU.max).then_inc(clipped, 1)
                dve.wait_ge(rooted, 1)
                link(nc.vector.reciprocal(deg[:], deg[:]))
                dve.wait_ge(loaded, 32)

                def body(t, s, turn):
                    dve.wait_ge(tr.made, t + 1)
                    nc.vector.scalar_tensor_tensor(tile(g, t), ps_out[:, s, 0:D], deg[:, bass.ds(t, 1)], bias[:],
                                                   ALU.mult, ALU.add).then_inc(done, 1)
                node_tiles(dve, body)
                dve.wait_ge(done, NT)
                link(nc.vector.tensor_scalar(g, g, 0.0, None, ALU.max))
                link(nc.vector.tensor_tensor(x, x, g, ALU.add))


def attention_tables(nc, c, w, h, q, dram):
    with phase(nc, "l3pre") as p:
        wt = p.sb("wt", [P, 3, D])
        kv = p.sb("kv", [P, 2, 2 * D])
        tr = TurnedRows(p, nc, c, h)
        ps_out = [p.ps("ps_out0", [P, 512]), p.ps("ps_out1", [P, 512])]
        loaded, q_taken, kv_taken = (p.sem(n) for n in ("loaded", "q_taken", "kv_taken"))
        stored = [p.sem("stored0"), p.sem("stored1")]
        with nc.Block() as block:
            @block.sync
            def _(sp):
                for i, name in enumerate(("L3_gnn_Wq", "L3_gnn_Wk", "L3_gnn_Wv")):
                    sp.dma_start(wt[:, i, :], w[name]).then_inc(loaded, 16)

                def store(t, s, turn):
                    sp.wait_ge(kv_taken, t + 1)
                    sp.dma_start(dram["kv"][bass.ds(t, 1)].rearrange("t p f -> (t p) f"), kv[:, s]).then_inc(stored[s], 16)
                node_tiles(sp, store)
                sp.wait_ge(stored[0], 16 * (NT // 2 + 1))
                sp.wait_ge(stored[1], 16 * (NT // 2))

            @block.scalar
            def _(act):
                def body(t, s, turn):
                    tr.copy(act, t, s)
                    act.wait_ge(kv_taken, t + 1)
                    nc.scalar.activation(tile(q, t), ps_out[s][:, 0:D], ACT.Copy, scale=0.25).then_inc(q_taken, 1)
                node_tiles(act, body)

            @block.gpsimd
            def _(pool):
                node_tiles(pool, lambda t, s, turn: tr.stage(pool, t, s))

            @block.tensor
            def _(pe):
                pe.wait_ge(loaded, 48)

                def body(t, s, turn):
                    tr.turn(pe, t, s)
                    pe.wait_ge(tr.copied, t + 1)
                    if known(t, 2):
                        pe.wait_ge(q_taken, t - 1)
                        pe.wait_ge(kv_taken, t - 1)
                    nc.tensor.matmul(ps_out[s][:, 0:3 * D], tr.rows[:, s, 0, :], wt[:], start=True, stop=True).then_inc(tr.made, 1)
                node_tiles(pe, body)

            @block.vector
            def _(dve):
                def body(t, s, turn):
                    dve.wait_ge(tr.made, t + 1)
                    if known(t, 2):
                        dve.wait_ge(stored[s], turn * 16)
                    nc.vector.tensor_copy(kv[:, s], ps_out[s][:, D:3 * D]).then_inc(kv_taken, 1)
                node_tiles(dve, body)


def attention_output(nc, c, w, h, acc, g, out):
    with phase(nc, "l3post") as p:
        wt, bias = p.sb("wt", [P, D]), p.sb("bias", [P, D])
        tr = TurnedRows(p, nc, c, g)
        ps_out = p.ps("ps_out", [P, 2, 512])
        loaded, steps, mixed, done = (p.sem(n) for n in ("loaded", "steps", "mixed", "done"))
        acc4 = acc.rearrange("p (t h w) -> p t h w", h=8, w=17)
        with nc.Block() as block:
            @block.sync
            def _(sp):
                sp.dma_start(wt[:], w["L3_gnn_Wo"]).then_inc(loaded, 16)
                sp.dma_start(bias[:], row_of(w["L3_gnn_bo"])).then_inc(loaded, 16)

            @block.scalar
            def _(act):
                node_tiles(act, lambda t, s, turn: tr.copy(act, t, s))

            @block.gpsimd
            def _(pool):
                pool.wait_ge(mixed, 1)
                node_tiles(pool, lambda t, s, turn: tr.stage(pool, t, s))

            @block.tensor
            def _(pe):
                pe.wait_ge(loaded, 32)

                def body(t, s, turn):
                    tr.turn(pe, t, s)
                    pe.wait_ge(tr.copied, t + 1)
                    if known(t, 2):
                        pe.wait_ge(done, t - 1)
                    nc.tensor.matmul(ps_out[:, s, 0:D], tr.rows[:, s, 0, :], wt[:], start=True, stop=True).then_inc(tr.made, 1)
                node_tiles(pe, body)

            @block.vector
            def _(dve):
                link = Chain(dve, steps)
                z = acc4[:, :, :, 16]
                link(nc.vector.tensor_scalar(z, z, 1e-6, None, ALU.add))
                link(nc.vector.reciprocal(z, z))
                nc.vector.tensor_tensor(g.rearrange("p t (h f) -> p t h f", f=16), acc4[:, :, :, 0:16],
                                        bcast(z, [P, NT, 8, 16]), ALU.mult).then_inc(mixed, 1)
                dve.wait_ge(loaded, 32)
                link(nc.vector.tensor_tensor(out, h, bias[:].unsqueeze(1).broadcast_to([P, NT, D]), ALU.add))

                def body(t, s, turn):
                    dve.wait_ge(tr.made, t + 1)
                    nc.vector.tensor_tensor(tile(out, t), tile(out, t), ps_out[:, s, 0:D], ALU.add).then_inc(done, 1)
                node_tiles(dve, body)


def batch_norm(nc, name, c, weight, bias, x, square, add_to=None):
    with phase(nc, name) as p:
        wr, br, mean, scale = (p.sb(n, [P, D]) for n in ("wr", "br", "mean", "scale"))
        slab = p.sb("slab", [P, 2, D])
        ps_mean, ps_var = p.ps("ps_mean", [P, 512]), p.ps("ps_var", [P, 512])
        loaded, steps, mean_made, centred, squared, var_made, var_ready, rooted = (
            p.sem(n) for n in ("loaded", "steps", "mean_made", "centred", "squared", "var_made", "var_ready", "rooted"))

        def rows(ap):
            return ap.unsqueeze(1).broadcast_to([P, NT, D])

        with nc.Block() as block:
            @block.sync
            def _(sp):
                sp.dma_start(wr[:], row_of(weight)).then_inc(loaded, 16)
                sp.dma_start(br[:], row_of(bias)).then_inc(loaded, 16)

            @block.tensor
            def _(pe):
                def column_sums(ps, v):
                    nc.tensor.matmul(ps[:, 0:D], c["ones_last"], v[:, NT - 1, :], start=True, stop=False)
                    with pe.Fori(0, NT - 2) as t:
                        nc.tensor.matmul(ps[:, 0:D], c["ones"], tile(v, t), start=False, stop=False)
                    return nc.tensor.matmul(ps[:, 0:D], c["ones"], v[:, NT - 2, :], start=False, stop=True)
                column_sums(ps_mean, x).then_inc(mean_made, 1)
                pe.wait_ge(squared, 1)
                column_sums(ps_var, square).then_inc(var_made, 1)

            @block.scalar
            def _(act):
                act.wait_ge(centred, 1)
                nc.scalar.activation(square, x, ACT.Square).then_inc(squared, 1)
                act.wait_ge(var_ready, 1)
                nc.scalar.activation(scale[:], scale[:], ACT.Sqrt).then_inc(rooted, 1)

            @block.vector
            def _(dve):
                link = Chain(dve, steps)
                dve.wait_ge(mean_made, 1)
                link(nc.vector.tensor_scalar(mean[:], ps_mean[:, 0:D], 1.0 / N, None, ALU.mult))
                nc.vector.tensor_tensor(x, x, rows(mean[:]), ALU.subtract).then_inc(centred, 1)
                dve.wait_ge(var_made, 1)
                nc.vector.tensor_scalar(scale[:], ps_var[:, 0:D], 1.0 / N, LN_EPS, ALU.mult, ALU.add).then_inc(var_ready, 1)
                dve.wait_ge(rooted, 1)
                link(nc.vector.reciprocal(scale[:], scale[:]))
                dve.wait_ge(loaded, 32)
                link(nc.vector.tensor_tensor(scale[:], scale[:], wr[:], ALU.mult))
                link(nc.vector.tensor_tensor(x, x, rows(scale[:]), ALU.mult))
                link(nc.vector.tensor_tensor(x, x, rows(br[:]), ALU.add))
                if add_to is not None:
                    link(nc.vector.tensor_tensor(add_to, add_to, x, ALU.add))


def graph_layers(nc, w, consts, out):
    dram = {
        "blocks": nc.dram_tensor("visit_blocks", (NV,), I32).ap(),
        "feat": nc.dram_tensor("visit_features", (NV, 5, GE), BF16).ap(),
        "flag": nc.dram_tensor("visit_flags", (NV, GE), F32).ap(),
        "kv_typed": nc.dram_tensor("kv_typed", (NT, P, R * 2 * D), F32).ap(),
        "pre": nc.dram_tensor("pre_rows", (P, NT, D), F32).ap(),
        "gat": nc.dram_tensor("gat_rows", (NP, 132), F32).ap(),
        "conv": nc.dram_tensor("conv_rows", (NP, D + 1), F32).ap(),
        "kv": nc.dram_tensor("kv_rows", (NT, P, 2 * D), F32).ap(),
    }
    with ExitStack() as ctx:
        def sb(name, shape, dt=F32):
            return ctx.enter_context(nc.sbuf_tensor(name, shape, dt))

        x = sb("x", [P, NT, D])
        top, a_dst, out_deg = sb("top", [P, NT * 4]), sb("a_dst", [P, NT * 4]), sb("out_deg", [P, NT])
        typed, kinds = sb("typed", [P, NT, T]), sb("kinds", [P, NT], I32)
        ident, ones, ones_last = sb("ident", [P, P]), sb("ones", [P, P]), sb("ones_last", [P, P])
        col_f, col_feat = sb("col_f", [5, P]), sb("col_feat", [5, P], BF16)
        iota_f, iota_bf = sb("iota_f", [P, P]), sb("iota_bf", [P, P], BF16)
        res = {
            "blocks": sb("block_row", [1, NV], I32), "top": top,
            "idx_typed": sb("idx_typed", [P, NV, G], I32), "idx_src": sb("idx_src", [P, NV, G], I32),
            "last": sb("last_cols", [P, NV, G]),
            "src_lo": sb("src_lo", [P, NV * G]), "src_hi": sb("src_hi", [P, NV * G]),
        }
        c = {"ident": ident[:], "col_feat": col_feat[:], "iota_bf": iota_bf[:], "ones": ones[:], "ones_last": ones_last[:],
             "visit_ids": consts["visit_ids"], "group_ids": consts["group_ids"]}

        with phase(nc, "load") as p:
            loaded, steps = p.sem("loaded"), p.sem("steps")
            with nc.Block() as block:
                @block.sync
                def _(sp):
                    sp.dma_start(x[:], w["x"]).then_inc(loaded, 16)
                    sp.dma_start(kinds[:], w["node_type_4"]).then_inc(loaded, 16)
                    sp.dma_start(ident[:], consts["ident"]).then_inc(loaded, 16)
                    sp.dma_start(col_f[:], consts["col_feat"]).then_inc(loaded, 16)
                    sp.dma_start(iota_f[:], consts["iota"].broadcast_to([P, P])).then_inc(loaded, 16)
                    sp.dma_start(ones_last[:], consts["ones_last"]).then_inc(loaded, 16)
                    sp.wait_ge(loaded, 96)

                @block.vector
                def _(dve):
                    link = Chain(dve, steps)
                    link(nc.vector.memset(ones[:], 1.0))
                    link(nc.vector.memset(top[:], -BIG))
                    dve.wait_ge(loaded, 96)
                    link(nc.vector.tensor_copy(col_feat[:], col_f[:]))
                    link(nc.vector.tensor_copy(iota_bf[:], iota_f[:]))
                    for y in range(T):
                        link(nc.vector.tensor_scalar(typed[:, :, y], kinds[:], float(y), None, ALU.is_equal))

        edge = {"ends": w["group_ends"], "dst": w["dst"], "src": w["src"], "et": w["edge_type_8"]}
        plan_visits(nc, c, edge, dram, res)

        h, q = sb("h", [P, NT, D]), sb("q", [P, NT, D])
        sums = sb("sums", [P, NT * 136])
        square = sums[:, 0:NT * D].rearrange("p (t d) -> p t d", d=D)

        def clear_sums():
            with phase(nc, "clear%d" % len(cleared)) as p:
                cleared.append(1)
                with nc.Block() as block:
                    @block.vector
                    def _(dve):
                        nc.vector.memset(sums[:], 0.0).then_inc(p.sem("zeroed"), 1)
        cleared = []

        norm_phase(nc, "ln0", x[:], h[:], square, relu=True)
        typed_tables(nc, c, w, h[:], typed[:], q[:], dram)
        clear_sums()
        q2 = q[:].rearrange("p t d -> p (t d)")
        edge_pass(nc, "edges0", c, dram, res, dram["kv_typed"].rearrange("t p (r f) -> (t p r) f", r=R), res["idx_typed"][:],
                  2 * D, 4, True, True, sums[:, 0:NT * 132], q=q2)
        typed_output(nc, c, w, x[:], h[:], typed[:], sums[:, 0:NT * 132], q[:], dram)

        norm_phase(nc, "ln1", x[:], h[:], square, relu=True)
        for_rows(nc, "ln1g", w["L1_gnn_ln1_g"], w["L1_gnn_ln1_b"], h[:], q[:], square)
        gat_tables(nc, c, w, q[:], sums[:, 0:NT * 132], top[:], a_dst[:], dram)
        edge_pass(nc, "edges1", c, dram, res, dram["gat"], res["idx_src"][:], 132, 4, False, True, sums[:, 0:NT * 132],
                  q=a_dst[:], hist=out_deg[:])
        gat_output(nc, c, w, h[:], sums[:, 0:NT * 132], q[:])
        for_rows(nc, "ln2g", w["L1_gnn_ln2_g"], w["L1_gnn_ln2_b"], q[:], h[:], square, add=x[:])
        feed_forward(nc, "ffn1", c, w["L1_gnn_w1"], w["L1_gnn_b1"], w["L1_gnn_w2"], w["L1_gnn_b2"], ACT.Gelu, h[:], x[:])

        norm_phase(nc, "ln2", x[:], h[:], square, relu=True)
        conv = sums[:, 0:NT * (D + 1)]
        conv3 = conv.rearrange("p (t f) -> p t f", t=NT)
        conv_table(nc, h[:], out_deg[:], conv3, dram)
        clear_sums()
        edge_pass(nc, "edges2", c, dram, res, dram["conv"], res["idx_src"][:], D + 1, 0, False, False, conv)
        conv_output(nc, c, w, x[:], conv3, q[:])

        norm_phase(nc, "ln3", x[:], h[:], square, relu=True)
        attention_tables(nc, c, w, h[:], q[:], dram)
        clear_sums()
        edge_pass(nc, "edges3", c, dram, res, dram["kv"].rearrange("t p f -> (t p) f"), res["idx_src"][:], 2 * D, 8, True, False,
                  sums[:], q=q2)
        hn = square
        attention_output(nc, c, w, h[:], sums[:], q[:], h[:])
        batch_norm(nc, "bn1", c, w["L3_gnn_bn1_w"], w["L3_gnn_bn1_b"], h[:], square)
        with phase(nc, "copy3") as p:
            with nc.Block() as block:
                @block.vector
                def _(dve):
                    nc.vector.tensor_copy(q[:], h[:]).then_inc(p.sem("copied"), 1)
        feed_forward(nc, "ffn3", c, w["L3_gnn_W1"], w["L3_gnn_b1"], w["L3_gnn_W2"], w["L3_gnn_b2"], ACT.Relu, h[:], q[:])
        batch_norm(nc, "bn2", c, w["L3_gnn_bn2_w"], w["L3_gnn_bn2_b"], q[:], square, add_to=x[:])

        with phase(nc, "store") as p:
            stored = p.sem("stored")
            with nc.Block() as block:
                @block.sync
                def _(sp):
                    sp.dma_start(out[0:(NT - 1) * P].rearrange("(t p) d -> p t d", p=P), x[:, 0:NT - 1, :]).then_inc(stored, 16)
                    sp.dma_start(out[(NT - 1) * P:N], x[0:TAIL, NT - 1, :]).then_inc(stored, 16)
                    sp.wait_ge(stored, 32)


def for_rows(nc, name, gamma, beta, x, out, square, add=None):
    with phase(nc, name) as p:
        g, b = p.sb("gamma", [P, D]), p.sb("beta", [P, D])
        ln = LayerNorm(p, x, out, square, False, g[:], b[:])
        loaded = p.sem("loaded")
        with nc.Block() as block:
            @block.sync
            def _(sp):
                sp.dma_start(g[:], row_of(gamma)).then_inc(loaded, 16)
                sp.dma_start(b[:], row_of(beta)).then_inc(loaded, 16)

            @block.vector
            def _(dve):
                dve.wait_ge(loaded, 32)
                ln.vector(nc, dve)
                if add is not None:
                    nc.vector.tensor_tensor(add, add, x, ALU.add).then_inc(p.sem("added"), 1)

            @block.scalar
            def _(act):
                ln.scalar(nc, act)


def kernel(**inputs):
    import concourse.bacc as _bacc
    from concourse.bass_utils import run_bass_kernel_spmd as _run

    arrays = {k: np.ascontiguousarray(v) for k, v in inputs.items()}

    def nodes(a, fill=0):
        pad = np.full((NP - N,) + a.shape[1:], fill, a.dtype)
        return np.ascontiguousarray(np.concatenate([a, pad]).reshape((NT, P) + a.shape[1:]).swapaxes(0, 1))

    def groups(a, fill):
        return np.concatenate([a, np.full(((NG + 1) * GE - E,), fill, a.dtype)]).reshape(NG + 1, GE)

    arrays["x"] = nodes(arrays["x"])
    arrays["node_type_4"] = nodes(arrays["node_type_4"])
    arrays["dst"] = groups(arrays["dst"], NP - 1)
    arrays["src"] = groups(arrays["src"], NP - 1)
    arrays["edge_type_8"] = groups(arrays["edge_type_8"], 0)
    arrays["group_ends"] = np.ascontiguousarray(arrays["dst"][:NG, [0, GE - 1]].T)
    for name in ("L3_gnn_Wq", "L3_gnn_Wk", "L3_gnn_Wv", "L3_gnn_Wo", "L3_gnn_W1", "L3_gnn_W2"):
        arrays[name] = np.ascontiguousarray(arrays[name].T)
    for name in ("L1_gnn_b1", "L3_gnn_b1"):
        arrays[name] = np.ascontiguousarray(arrays[name].reshape(2, D).T)
    j = np.arange(P)
    consts = {
        "ident": np.eye(P, dtype=np.float32),
        "iota": np.arange(P, dtype=np.float32)[None],
        "ones_last": np.repeat((j < TAIL).astype(np.float32)[:, None], P, 1),
        "col_feat": np.stack([np.full(P, 128), np.ones(P), -2 * j, j * j // 128 * 128, j * j % 128]).astype(np.float32),
        "visit_ids": np.arange(NV, dtype=np.float32).reshape(VC, VP).T.copy(),
        "group_ids": np.arange(NG + 1, dtype=np.float32)[None],
    }
    nc = _bacc.Bacc("TRN2", target_bir_lowering=False, num_devices=1)
    feeds, w, cs = {}, {}, {}
    for pre, group, aps in (("in_", arrays, w), ("const_", consts, cs)):
        for name, a in group.items():
            feeds[pre + name] = a
            aps[name] = nc.dram_tensor(pre + name, a.shape, mybir.dt.from_np(a.dtype), kind="ExternalInput").ap()
    out = nc.dram_tensor("out_0_dram", (N, D), F32, kind="ExternalOutput").ap()
    graph_layers(nc, w, cs, out)
    r = _run(nc, [feeds], core_ids=[0])
    return r.results[0]["out_0_dram"]
```

```python
from contextlib import ExitStack, contextmanager

import numpy as np

import concourse.bass as bass
from concourse import mybir

ALU = mybir.AluOpType
ACT = mybir.ActivationFunctionType
AX = mybir.AxisListType
F32 = mybir.dt.float32
BF16 = mybir.dt.bfloat16
I32 = mybir.dt.int32

P = 128
N = 6250
NT = -(-N // P)
NP = NT * P
TAIL = N - (NT - 1) * P
E = 200000
G = 4
GE = G * P
NG = -(-E // GE)
NV = -(-(NG + NT - 1) // G) * G
VC = 4
VP = NV // VC
D = 128
R = 8
T = 4
BIG = 2.0 ** 100
LN_EPS = 1e-5
LAM = 0.3
SLOPE = 0.2


def bcast(ap, shape):
    return ap.unsqueeze(len(ap.shape)).broadcast_to(shape)


class Phase:

    def __init__(self, nc, name, ctx):
        self.nc, self.name, self.ctx, self.sems = nc, name, ctx, []

    def sb(self, name, shape, dt=F32):
        return self.ctx.enter_context(self.nc.sbuf_tensor(f"{self.name}_{name}", shape, dt))

    def ps(self, name, shape, dt=F32):
        return self.ctx.enter_context(self.nc.psum_tensor(f"{self.name}_{name}", shape, dt))

    def sem(self, name):
        self.sems.append(self.nc.alloc_semaphore(f"{self.name}_{name}"))
        return self.sems[-1]


@contextmanager
def phase(nc, name):
    with ExitStack() as ctx:
        p = Phase(nc, name, ctx)
        yield p
    nc.clear_and_free_semaphores(p.sems)
    nc.all_engine_barrier()


class Chain:

    def __init__(self, eng, sem):
        self.eng, self.sem, self.n = eng, sem, 0

    def __call__(self, ins):
        self.n += 1
        ins.then_inc(self.sem, 1)
        self.eng.wait_ge(self.sem, self.n)


def node_tiles(eng, body):
    body(0, 0, 0)
    body(1, 1, 0)
    with eng.Fori(1, NT // 2) as i:
        body(i * 2, 0, i)
        body(i * 2 + 1, 1, i)
    body(NT - 1, 0, NT // 2)


def known(t, least):
    return not isinstance(t, int) or t >= least


class LayerNorm:

    def __init__(self, p, x, out, square, relu, gamma=None, beta=None):
        self.x, self.out, self.square, self.relu, self.gamma, self.beta = x, out, square, relu, gamma, beta
        self.mean, self.var, self.rstd = (p.sb(n, [P, NT]) for n in ("mean", "var", "rstd"))
        self.centred, self.squared, self.var_ready, self.std_ready, self.steps, self.done = (
            p.sem(n) for n in ("ln_centred", "ln_squared", "ln_var", "ln_std", "ln_steps", "ln_done"))

    def vector(self, nc, dve):
        link = Chain(dve, self.steps)
        shape = [P, NT, D]
        link(nc.vector.reduce_sum(self.mean[:], self.x, AX.X))
        link(nc.vector.tensor_scalar(self.mean[:], self.mean[:], 1.0 / D, None, ALU.mult))
        nc.vector.tensor_tensor(self.out, self.x, bcast(self.mean[:], shape), ALU.subtract).then_inc(self.centred, 1)
        dve.wait_ge(self.squared, 1)
        link(nc.vector.reduce_sum(self.var[:], self.square, AX.X))
        nc.vector.tensor_scalar(self.var[:], self.var[:], 1.0 / D, LN_EPS, ALU.mult, ALU.add).then_inc(self.var_ready, 1)
        dve.wait_ge(self.std_ready, 1)
        link(nc.vector.reciprocal(self.rstd[:], self.var[:]))
        if self.relu:
            link(nc.vector.tensor_scalar(self.out, self.out, 0.0, None, ALU.max))
        last = nc.vector.tensor_tensor(self.out, self.out, bcast(self.rstd[:], shape), ALU.mult)
        if self.gamma is not None:
            link(last)
            rows = [P, NT, D]
            link(nc.vector.tensor_tensor(self.out, self.out, self.gamma.unsqueeze(1).broadcast_to(rows), ALU.mult))
            last = nc.vector.tensor_tensor(self.out, self.out, self.beta.unsqueeze(1).broadcast_to(rows), ALU.add)
        last.then_inc(self.done, 1)

    def scalar(self, nc, act):
        act.wait_ge(self.centred, 1)
        nc.scalar.activation(self.square, self.out, ACT.Square).then_inc(self.squared, 1)
        act.wait_ge(self.var_ready, 1)
        nc.scalar.activation(self.var[:], self.var[:], ACT.Sqrt).then_inc(self.std_ready, 1)


def plan_visits(nc, c, edge, dram, res):
    with phase(nc, "plan") as p:
        ends_i, ends_b, ends_f = p.sb("ends_i", [1, 2, NG], I32), p.sb("ends_b", [1, 2, NG], I32), p.sb("ends_f", [1, 2, NG])
        ones_row = p.sb("ones_row", [1, P])
        blk_first, n_blocks, csum, base, ones_g, junk = (
            p.sb(n, [P, NG]) for n in ("blk_first", "n_blocks", "csum", "base", "ones_g", "junk"))
        vis, tv, bv, shift = (p.sb(n, [VP, VC]) for n in ("vis", "tv", "bv", "shift"))
        tvi, bvi = p.sb("tvi", [VP, VC], I32), p.sb("bvi", [VP, VC], I32)
        git = p.sb("git", [P, NG])
        dst_g, src_g, et_g = (p.sb(n, [VP, VC, GE], I32) for n in ("dst_g", "src_g", "et_g"))
        dl = p.sb("dl", [VP, GE])
        sq, hi, lo = (p.sb(n, [VP, GE], I32) for n in ("sq", "hi", "lo"))
        feat = p.sb("feat", [VP, 2, 5, GE], BF16)
        last, ia, ib = (p.sb(n, [VP, 2, GE]) for n in ("last", "ia", "ib"))
        flag = p.sb("flag", [VP, 2, GE], BF16)
        ps_first, ps_last = p.ps("ps_first", [P, 512]), p.ps("ps_last", [P, 512])
        ps_t = [p.ps(n, [P, G, VP]) for n in ("ps_ta", "ps_tb", "ps_tc")]
        lo_i, hi_i, his = p.sb("lo_i", [P, NG * G + G], I32), p.sb("hi_i", [P, NG * G + G], I32), p.sb("his", [P, NG * G + G], I32)
        n_hist = (NG + 1) * G
        cols = [p.sb("cols_typed", [P, NV, G], I32), p.sb("cols_src", [P, NV, G], I32), p.sb("cols_last", [P, NV, G], BF16)]

        loaded, rows_ready, spread, steps, plan_ready, idx_stored = (
            p.sem(n) for n in ("loaded", "rows_ready", "spread", "steps", "plan_ready", "idx_stored"))
        gathered = [p.sem(f"gathered{k}") for k in range(VC)]
        made, stored, turned, taken = (p.sem(n) for n in ("made", "stored", "turned", "taken"))
        block_row_in = p.sem("block_row_in")

        with nc.Block() as block:
            @block.sync
            def _(sp):
                sp.dma_start(ends_i[:], edge["ends"].rearrange("(o k) g -> o k g", o=1)).then_inc(loaded, 16)
                sp.dma_start(vis[:], c["visit_ids"]).then_inc(loaded, 16)
                sp.dma_start(git[:], c["group_ids"][:, 0:NG].broadcast_to([P, NG])).then_inc(loaded, 16)
                sp.dma_start(his[:, 0:n_hist], edge["src"].rearrange("g e -> (g e)").rearrange("(p j) -> p j", p=P)).then_inc(loaded, 16)
                sp.wait_ge(plan_ready, 1)
                with nc.allow_non_contiguous_dma(reason="a few hundred block numbers, once"):
                    sp.dma_start(dram["blocks"].rearrange("(c p) -> p c", c=VC), bvi[:]).then_inc(idx_stored, 16)
                sp.wait_ge(idx_stored, 16)
                sp.dma_start(res["blocks"][:], dram["blocks"].rearrange("(o v) -> o v", o=1)).then_inc(block_row_in, 16)
                for k in range(VC):
                    sp.wait_ge(made, k + 1)
                    sp.dma_start(dram["feat"][k * VP:(k + 1) * VP], feat[:, k % 2]).then_inc(stored, 16)
                    sp.dma_start(dram["flag"][k * VP:(k + 1) * VP], flag[:, k % 2]).then_inc(stored, 16)
                    sp.wait_ge(stored, 32 * (k + 1))
                sp.wait_ge(block_row_in, 16)
                sp.wait_ge(taken, VC)
                for col, name in zip(cols, ("idx_typed", "idx_src", "last")):
                    sp.dma_start(dram[name], col[:]).then_inc(stored, 16)
                sp.wait_ge(stored, 32 * VC + 48)

            @block.gpsimd
            def _(pool):
                pool.wait_ge(plan_ready, 1)
                for k in range(VC):
                    for out, tab in ((dst_g, "dst"), (src_g, "src"), (et_g, "et")):
                        pool.indirect_dma_start(out[:, k, :], None, edge[tab],
                                                bass.IndirectOffsetOnAxis(ap=tvi[:, k:k + 1], axis=0)).then_inc(gathered[k], 16)

            @block.tensor
            def _(pe):
                pe.wait_ge(rows_ready, 1)
                nc.tensor.matmul(ps_first[:, 0:NG], ones_row[:], ends_f[:, 0, :], start=True, stop=True)
                nc.tensor.matmul(ps_last[:, 0:NG], ones_row[:], ends_f[:, 1, :], start=True, stop=True).then_inc(spread, 1)
                for k in range(VC):
                    pe.wait_ge(made, k + 1)
                    if k:
                        pe.wait_ge(taken, k)
                    for ps, rows in zip(ps_t, (ia, ib, last)):
                        for g in range(G):
                            mm = nc.tensor.transpose(ps[:, g, :], rows[:, k % 2, g * P:(g + 1) * P], c["ident"][0:VP, 0:VP])
                    mm.then_inc(turned, 1)

            @block.vector
            def _(dve):
                link = Chain(dve, steps)
                link(nc.vector.memset(ones_row[:], 1.0))
                link(nc.vector.memset(ones_g[:], 1.0))
                dve.wait_ge(loaded, 64)
                link(nc.vector.tensor_scalar(ends_b[:], ends_i[:], 7, None, ALU.logical_shift_right))
                nc.vector.tensor_copy(ends_f[:], ends_b[:]).then_inc(rows_ready, 1)
                link(nc.vector.tensor_scalar(lo_i[:, 0:n_hist], his[:, 0:n_hist], P - 1, None, ALU.bitwise_and))
                link(nc.vector.tensor_scalar(hi_i[:, 0:n_hist], his[:, 0:n_hist], 7, None, ALU.logical_shift_right))
                link(nc.vector.memset(res["src_lo"][:], -1.0))
                link(nc.vector.memset(res["src_hi"][:], -1.0))
                link(nc.vector.tensor_copy(res["src_lo"][:, 0:n_hist], lo_i[:, 0:n_hist]))
                link(nc.vector.tensor_copy(res["src_hi"][:, 0:n_hist], hi_i[:, 0:n_hist]))
                dve.wait_ge(spread, 1)
                link(nc.vector.tensor_copy(blk_first[:], ps_first[:, 0:NG]))
                link(nc.vector.scalar_tensor_tensor(n_blocks[:], ps_last[:, 0:NG], 1.0, blk_first[:], ALU.add, ALU.subtract))
                link(nc.vector.tensor_tensor_scan(csum[:], ones_g[:], n_blocks[:], 0.0, ALU.mult, ALU.add))
                link(nc.vector.tensor_tensor(base[:], blk_first[:], csum[:], ALU.subtract))
                link(nc.vector.tensor_tensor(base[:], base[:], n_blocks[:], ALU.add))
                for k in range(VC):
                    link(nc.vector.tensor_scalar(junk[0:VP], csum[0:VP], vis[:, k:k + 1], 0.0, ALU.is_le, ALU.add,
                                                 accum_out=tv[:, k:k + 1]))
                    link(nc.vector.scalar_tensor_tensor(junk[0:VP], git[0:VP], tv[:, k:k + 1], base[0:VP],
                                                        ALU.is_equal, ALU.mult, accum_out=bv[:, k:k + 1]))
                link(nc.vector.tensor_tensor(bv[:], bv[:], vis[:], ALU.add))
                link(nc.vector.tensor_scalar(bv[:], bv[:], float(NT - 1), 0.0, ALU.min, ALU.max))
                link(nc.vector.tensor_scalar(shift[:], bv[:], -float(P), None, ALU.mult))
                link(nc.vector.tensor_copy(tvi[:], tv[:]))
                nc.vector.tensor_copy(bvi[:], bv[:]).then_inc(plan_ready, 1)
                dve.wait_ge(plan_ready, 1)

                def take(k):
                    dve.wait_ge(turned, k + 1)
                    vs = slice(k * VP, (k + 1) * VP)
                    for ps, out in zip(ps_t, cols):
                        ins = nc.vector.tensor_copy(out[:, vs, :], ps[:].rearrange("p g v -> p v g"))
                    ins.then_inc(taken, 1)

                for k in range(VC):
                    s = k % 2
                    dve.wait_ge(gathered[k], 48)
                    if k >= 2:
                        dve.wait_ge(stored, 32 * (k - 1))
                    link(nc.vector.tensor_scalar(dl[:], dst_g[:, k, :], shift[:, k:k + 1], -1.0, ALU.add, ALU.max))
                    link(nc.vector.tensor_scalar(dl[:], dl[:], float(P), None, ALU.min))
                    link(nc.vector.tensor_tensor(sq[:], dl[:], dl[:], ALU.mult))
                    link(nc.vector.tensor_scalar(hi[:], sq[:], 7, None, ALU.logical_shift_right))
                    link(nc.vector.tensor_scalar(lo[:], sq[:], P - 1, None, ALU.bitwise_and))
                    link(nc.vector.tensor_copy(feat[:, s, 0, :], hi[:]))
                    link(nc.vector.tensor_copy(feat[:, s, 1, :], lo[:]))
                    link(nc.vector.tensor_copy(feat[:, s, 2, :], dl[:]))
                    link(nc.vector.memset(feat[:, s, 3:5, :], 1.0))
                    link(nc.vector.tensor_tensor(last[:, s, 0:GE - 1], dst_g[:, k, 1:GE], dst_g[:, k, 0:GE - 1], ALU.not_equal))
                    link(nc.vector.tensor_scalar(flag[:, s, 1:GE], last[:, s, 0:GE - 1], -BIG, None, ALU.mult))
                    link(nc.vector.memset(flag[:, s, 0:1], -BIG))
                    link(nc.vector.memset(last[:, s, GE - 1:GE], 1.0))
                    link(nc.vector.tensor_copy(ib[:, s, :], src_g[:, k, :]))
                    link(nc.vector.tensor_scalar(ia[:, s, :], ib[:, s, :], float(R), None, ALU.mult))
                    nc.vector.tensor_tensor(ia[:, s, :], ia[:, s, :], et_g[:, k, :], ALU.add).then_inc(made, 1)
                    take(k)


def edge_pass(nc, name, c, dram, res, table, idx, width, heads, dot, softmax, acc, q=None, hist=None):
    hd = D // heads if heads else D
    hw = hd + 1
    aw = heads * hw if heads else D + 1
    weighted = heads > 0
    RING = 8
    SLOTS = 4
    with phase(nc, name) as p:
        rows = p.sb("rows", [P, RING, G, width])
        idx_r = p.sb("idx_r", [P, RING, G], I32)
        feat_r = p.sb("feat_r", [5, SLOTS, GE], BF16)
        flag_r = p.sb("flag_r", [4, SLOTS, GE], BF16)
        last_r = p.sb("last_r", [P, SLOTS, G], BF16)
        pick = p.sb("pick", [P, RING, GE])
        pick_t = p.sb("pick_t", [P, 2, GE]) if dot else None
        pick_b = p.sb("pick_b", [P, SLOTS, GE], BF16) if softmax else None
        pick_tb = p.sb("pick_tb", [P, SLOTS, GE], BF16) if softmax else None
        prod = p.sb("prod", [P, GE])
        logit = p.sb("logit", [P, SLOTS, G * max(heads, 1)])
        gap = p.sb("gap", [P, G * max(heads, 1)])
        run = p.sb("run", [4, GE])
        ends = p.sb("ends", [P, G, 4])
        ends_hi, ends_lo = p.sb("ends_hi", [P, G, 5], BF16), p.sb("ends_lo", [P, G, 5], BF16)
        top_hi, top_lo = p.sb("top_hi", [P, 4], BF16), p.sb("top_lo", [P, 4], BF16)
        absent = p.sb("absent", [P, 1])
        turns = p.sb("turns", [1, 2])
        top = p.sb("top", [P, 4])
        drop, fade = p.sb("drop", [P, 2, 4]), p.sb("fade", [P, 2, 4])
        wv = p.sb("wv", [P, 2, G, aw])
        lo_hot, hi_hot = p.sb("lo_hot", [P, 2, G, P], BF16), p.sb("hi_hot", [P, 2, G, NT], BF16)

        ps_pick, ps_pick_t = p.ps("ps_pick", [P, GE]), p.ps("ps_pick_t", [P, GE])
        ps_turn, ps_back = p.ps("ps_turn", [4, GE]), p.ps("ps_back", [P, 512])
        ps_ref = p.ps("ps_ref", [P, 512]) if softmax else None
        ps_top, ps_sum = p.ps("ps_top", [P, 512]), p.ps("ps_sum", [P, 512])
        ps_hist = p.ps("ps_hist", [P, 512]) if hist is not None else None
        ps_q = p.ps("ps_q", [P, GE]) if dot or not softmax else ps_top[:, 256:512]

        idx_in = [p.sem(f"idx_in{k}") for k in range(RING)]
        feat_in = [p.sem(f"feat_in{k}") for k in range(SLOTS)]
        seg_in = [p.sem(f"seg_in{k}") for k in range(SLOTS)]
        rows_in = [p.sem(f"rows_in{k}") for k in range(RING)]
        (squares_done, pick_done, pick_t_done, q_done, prod_done, logit_done, turn_done, run_done, back_done, marked_done,
         top_part, absent_done, top_done, drop_done, ref_done, gap_part, gap_done, weight_done, wv_done, fade_done,
         sum_done, faded, acc_done, one, hot_done, hist_done, top_kept, gate, ends_done, ends_high, top_high,
         top_split, pick_b_done, pick_tb_done, edge_logit, zeroed) = (p.sem(n) for n in (
            "squares_done", "pick_done", "pick_t_done", "q_done", "prod_done", "logit_done", "turn_done", "run_done",
            "back_done", "marked_done", "top_part", "absent_done", "top_done", "drop_done", "ref_done", "gap_part",
            "gap_done", "weight_done", "wv_done", "fade_done", "sum_done", "faded", "acc_done", "one", "hot_done",
            "hist_done", "top_kept", "gate", "ends_done", "ends_high", "top_high", "top_split", "pick_b_done", "pick_tb_done", "edge_logit", "zeroed"))

        def visits(eng, body, ahead):
            for i in range(-ahead, RING):
                body(i, i % RING, i // RING)
            with eng.Fori(1, NV // RING - 1) as it:
                for k in range(RING):
                    body(it * RING + k, k, it)
            for i in range(NV - RING, NV + 3):
                body(i, i % RING, i // RING)

        def at(i, k, it, d):
            if isinstance(i, int):
                if not 0 <= i + d < NV:
                    return None
                u, s, t = i + d, (i + d) % RING, (i + d) // RING
            else:
                u, s, t = i + d, (k + d) % RING, it + (k + d) // RING
            return u, s, t, s % SLOTS, t * (RING // SLOTS) + s // SLOTS

        def up_to(count):
            return min(count, NV) if isinstance(count, int) else count

        def block_of(eng, u):
            return eng.value_load(res["blocks"][0:1, bass.ds(u, 1)], min_val=0, max_val=NT - 1)

        wv4 = wv[:].rearrange("p s g (h w) -> p s g h w", w=hw) if weighted else None

        with nc.Block() as block:
            @block.sync
            def _(sp):
                def body(i, k, it):
                    if v := at(i, k, it, 0):
                        u, s, t, _, _ = v
                        if known(u, RING):
                            sp.wait_ge(rows_in[s], t * 64)
                        sp.dma_start(idx_r[:, s, :], idx[:, bass.ds(u, 1), :].rearrange("p v g -> p (v g)")).then_inc(idx_in[s], 16)
                    if (v := at(i, k, it, -3)) is None:
                        return
                    u, s, t, s4, t4 = v
                    if known(u, SLOTS):
                        sp.wait_ge(squares_done, u - (SLOTS - 1))
                    sp.dma_start(feat_r[:, s4, :], dram["feat"][bass.ds(u, 1)].rearrange("v f e -> (v f) e")).then_inc(feat_in[s4], 16)
                    if softmax:
                        if known(u, SLOTS):
                            sp.wait_ge(run_done, u - (SLOTS - 1))
                            sp.wait_ge(marked_done, u - (SLOTS - 1))
                        sp.dma_start(flag_r[:, s4, :], dram["flag"][bass.ds(u, 1), :].broadcast_to([4, GE])).then_inc(seg_in[s4], 16)
                        sp.dma_start(last_r[:, s4, :], dram["last"][:, bass.ds(u, 1), :].rearrange("p v g -> p (v g)")).then_inc(seg_in[s4], 16)
                visits(sp, body, 0)

            @block.gpsimd
            def _(pool):
                nc.gpsimd.memset(turns[:], 0.0).then_inc(one, 1)
                pool.wait_ge(one, 1)

                def body(i, k, it):
                    if (v := at(i, k, it, 0)) is None:
                        return
                    u, s, t, _, _ = v
                    pool.wait_ge(idx_in[s], t * 16 + 16)
                    if known(u, RING):
                        pool.wait_ge(wv_done if weighted else sum_done, u - (RING - 1))
                    if known(u, 1):
                        pool.wait_ge(gate, u)
                    nc.gpsimd.tensor_tensor(turns[:, 0:1], turns[:, 1:2], turns[:, 1:2], ALU.add).then_inc(gate, 1)
                    for g in range(G):
                        pool.indirect_dma_start(rows[:, s, g, :], None, table,
                                                bass.IndirectOffsetOnAxis(ap=idx_r[:, s, g:g + 1], axis=0)).then_inc(rows_in[s], 16)
                visits(pool, body, 0)

            @block.tensor
            def _(pe):
                if softmax:
                    pe.wait_ge(zeroed, 1)
                if hist is not None:
                    pe.wait_ge(hot_done, 1)
                    nc.tensor.matmul(ps_hist[:, 0:NT], lo_hot[:, 0, 0, :], hi_hot[:, 0, 0, :], start=True, stop=False,
                                     skip_group_check=True).then_inc(hist_done, 1)

                def squares(v):
                    u, s, t, s4, t4 = v
                    pe.wait_ge(feat_in[s4], t4 * 16 + 16)
                    if known(u, 1):
                        if weighted:
                            pe.wait_ge(pick_tb_done if softmax else pick_t_done, u)
                        pe.wait_ge(pick_done, u)
                    if weighted:
                        nc.tensor.matmul(ps_pick_t[:], c["col_feat"], feat_r[:, s4, :], start=True, stop=True)
                    for g in range(G):
                        mm = nc.tensor.matmul(ps_pick[:, g * P:(g + 1) * P], feat_r[:, s4, g * P:(g + 1) * P],
                                              c["col_feat"], start=True, stop=True)
                    mm.then_inc(squares_done, 1)

                def await_maxima(v):
                    u, s, t, s4, t4 = v
                    pe.wait_ge(run_done, u + 1)
                    if known(u, 1):
                        pe.wait_ge(marked_done, u)

                def turn_back(v):
                    u, s, t, s4, t4 = v
                    for g in range(G):
                        mm = nc.tensor.transpose(ps_back[:, g * 4:(g + 1) * 4], run[:, g * P:(g + 1) * P], c["ident"][0:4, 0:4])
                    mm.then_inc(back_done, 1)

                def spread_max(v):
                    u, s, t, s4, t4 = v
                    pe.wait_ge(top_split, u + 1)
                    pe.wait_ge(pick_tb_done, u + 1)
                    if known(u, 1):
                        pe.wait_ge(gap_part, u)
                    for g in range(G):
                        for part in (top_hi, top_lo):
                            mm = nc.tensor.matmul(ps_ref[:, g * 4:(g + 1) * 4], pick_tb[:, s4, g * P:(g + 1) * P], part[:],
                                                  start=part is top_hi, stop=part is top_lo)
                    mm.then_inc(ref_done, 1)

                def spread_q(v, b):
                    u, s, t, s4, t4 = v
                    qw = D if dot else 12
                    pe.wait_ge(pick_t_done if dot else pick_tb_done, u + 1)
                    if known(u, 1):
                        pe.wait_ge(prod_done, u)
                    for g in range(G):
                        hot = pick_t[:, s % 2, g * P:(g + 1) * P] if dot else pick_tb[:, s4, g * P:(g + 1) * P]
                        mm = nc.tensor.matmul(ps_q[:, g * qw:(g + 1) * qw], hot,
                                              q[:, bass.ds(b * qw, qw)], start=True, stop=True)
                    mm.then_inc(q_done, 1)

                def turn_logits(v):
                    u, s, t, s4, t4 = v
                    pe.wait_ge(logit_done, u + 1)
                    if known(u, 1):
                        pe.wait_ge(run_done, u)
                    for g in range(G):
                        mm = nc.tensor.transpose(ps_turn[:, g * P:(g + 1) * P], logit[:, s4, g * 4:(g + 1) * 4], c["ident"])
                    mm.then_inc(turn_done, 1)

                def sum_rows(v):
                    u, s, t, s4, t4 = v
                    if weighted:
                        pe.wait_ge(wv_done, u + 1)
                    else:
                        pe.wait_ge(rows_in[s], t * 64 + 64)
                        pe.wait_ge(pick_done, u + 1)
                    if known(u, 1):
                        pe.wait_ge(acc_done, u)
                    for g in range(G):
                        rhs = wv[:, s % 2, g, :] if weighted else rows[:, s, g, :]
                        mm = nc.tensor.matmul(ps_sum[:, 0:aw], pick[:, s, g * P:(g + 1) * P], rhs, start=g == 0, stop=g == G - 1)
                    mm.then_inc(sum_done, 1)

                def block_max(v):
                    u, s, t, s4, t4 = v
                    pe.wait_ge(marked_done, u + 1)
                    if known(u, 1):
                        pe.wait_ge(top_done, u)
                    if not dot:
                        pe.wait_ge(prod_done, up_to(u + 2))
                    pe.wait_ge(pick_b_done, u + 1)
                    for g in range(G):
                        for part in (ends_hi, ends_lo):
                            mm = nc.tensor.matmul(ps_top[:, 0:5], pick_b[:, s4, g * P:(g + 1) * P], part[:, g, :],
                                                  start=g == 0 and part is ends_hi, stop=g == G - 1 and part is ends_lo)
                    mm.then_inc(top_part, 1)

                def count_sources(v):
                    u, s, t, s4, t4 = v
                    pe.wait_ge(hot_done, u + 2)
                    for g in range(G):
                        mm = nc.tensor.matmul(ps_hist[:, 0:NT], lo_hot[:, s % 2, g, :], hi_hot[:, s % 2, g, :],
                                              start=False, stop=False, skip_group_check=True)
                    mm.then_inc(hist_done, 1)

                def body(i, k, it):
                    after, now, before, earlier, oldest = (at(i, k, it, d) for d in (1, 0, -1, -2, -3))
                    if weighted and after:
                        block = block_of(pe, after[0])
                    if softmax and before:
                        await_maxima(before)
                    if after:
                        squares(after)
                    if softmax and before:
                        turn_back(before)
                    if oldest:
                        sum_rows(oldest)
                    if softmax and earlier:
                        spread_max(earlier)
                    if softmax and now:
                        turn_logits(now)
                    if hist is not None and before:
                        count_sources(before)
                    if softmax and before:
                        block_max(before)
                    if weighted and after:
                        spread_q(after, block)
                visits(pe, body, 1)

            @block.scalar
            def _(act):
                def one_hot(out, squares, done):
                    nc.scalar.activation(out, squares[:], ACT.Relu, bias=1.0, scale=-1.0).then_inc(done, 1)

                def shrink(v):
                    u, s, t, s4, t4 = v
                    act.wait_ge(drop_done, u + 1)
                    if known(u, 2):
                        act.wait_ge(acc_done, u - 1)
                    nc.scalar.activation(fade[:, s % 2, :], drop[:, s % 2, :], ACT.Exp).then_inc(fade_done, 1)

                def weights(v):
                    u, s, t, s4, t4 = v
                    act.wait_ge(gap_done, u + 1)
                    if known(u, 2):
                        act.wait_ge(sum_done, u - 1)
                    nc.scalar.activation(wv4[:, s % 2, :, :, hd], gap[:].rearrange("p (g h) -> p g h", g=G), ACT.Exp).then_inc(weight_done, 1)

                def body(i, k, it):
                    after, earlier = at(i, k, it, 1), at(i, k, it, -2)
                    if after:
                        u, s, t, s4, t4 = after
                        act.wait_ge(squares_done, u + 1)
                        if dot:
                            if known(u, 2):
                                act.wait_ge(q_done, u - 1)
                            one_hot(pick_t[:, s % 2, :], ps_pick_t, pick_t_done)
                        if softmax:
                            if known(u, SLOTS):
                                act.wait_ge(ref_done, u - (SLOTS - 1))
                            one_hot(pick_tb[:, s4, :], ps_pick_t, pick_tb_done)
                    if softmax and earlier:
                        shrink(earlier)
                    if after:
                        if softmax:
                            if known(u, SLOTS):
                                act.wait_ge(top_part, u - (SLOTS - 1))
                            one_hot(pick_b[:, s4, :], ps_pick, pick_b_done)
                        if known(u, RING):
                            act.wait_ge(sum_done, u - (RING - 1))
                        one_hot(pick[:, s, :], ps_pick, pick_done)
                    if weighted and earlier:
                        weights(earlier)
                visits(act, body, 1)

            @block.vector
            def _(dve):
                if softmax:
                    nc.vector.memset(ends_lo[:, :, 4], 0.0).then_inc(zeroed, 1)
                if hist is not None:
                    nc.vector.memset(lo_hot[:, 0, 0, :], 0.0)
                    nc.vector.memset(hi_hot[:, 0, 0, :], 0.0).then_inc(hot_done, 1)

                def running_max(v):
                    u, s, t, s4, t4 = v
                    dve.wait_ge(seg_in[s4], t4 * 32 + 32)
                    dve.wait_ge(turn_done, u + 1)
                    nc.vector.tensor_tensor_scan(run[:], flag_r[:, s4, :], ps_turn[:], -BIG, ALU.add, ALU.max).then_inc(run_done, 1)

                def ends_a(v):
                    u, s, t, s4, t4 = v
                    dve.wait_ge(back_done, u + 1)
                    nc.vector.tensor_tensor(ends[:], ps_back[:, 0:4 * G].rearrange("p (g h) -> p g h", g=G),
                                            bcast(last_r[:, s4, :], [P, G, 4]), ALU.mult).then_inc(ends_done, 1)

                def ends_b(v):
                    u, s, t, s4, t4 = v
                    dve.wait_ge(ends_done, u + 1)
                    nc.vector.tensor_copy(ends_hi[:, :, 0:4], ends[:]).then_inc(ends_high, 1)

                def ends_c(v):
                    u, s, t, s4, t4 = v
                    dve.wait_ge(ends_high, u + 1)
                    nc.vector.tensor_copy(ends_hi[:, :, 4], last_r[:, s4, :])
                    nc.vector.tensor_tensor(ends_lo[:, :, 0:4], ends[:], ends_hi[:, :, 0:4], ALU.subtract).then_inc(marked_done, 1)

                def logits_a(v):
                    u, s, t, s4, t4 = v
                    dve.wait_ge(rows_in[s], t * 64 + 64)
                    dve.wait_ge(q_done, u + 1)
                    if known(u, 1):
                        dve.wait_ge(logit_done, u)
                    if dot:
                        nc.vector.tensor_tensor(prod[:].rearrange("p (g d) -> p g d", g=G), rows[:, s, :, 0:D],
                                                ps_q[:].rearrange("p (g d) -> p g d", g=G), ALU.mult).then_inc(prod_done, 1)
                    else:
                        nc.vector.reduce_sum(prod[:, 0:4 * G].rearrange("p (g h) -> p g h", g=G),
                                             ps_q[:, 0:12 * G].rearrange("p (g k h) -> p g h k", g=G, k=3), AX.X).then_inc(prod_done, 1)

                def logits_a2(v):
                    u, s, t, s4, t4 = v
                    if not dot:
                        dve.wait_ge(prod_done, u + 1)
                        nc.vector.tensor_tensor(prod[:, 4 * G:8 * G].rearrange("p (g h) -> p g h", g=G),
                                                rows[:, s].rearrange("p g (h w) -> p g h w", w=hw)[:, :, :, hd],
                                                prod[:, 0:4 * G].rearrange("p (g h) -> p g h", g=G), ALU.add).then_inc(edge_logit, 1)

                def logits_b(v):
                    u, s, t, s4, t4 = v
                    dve.wait_ge(prod_done, u + 1)
                    if known(u, SLOTS):
                        dve.wait_ge(gap_done, u - (SLOTS - 1))
                    if dot:
                        nc.vector.reduce_sum(logit[:, s4, :], prod[:].rearrange("p (k d) -> p k d", d=hd), AX.X).then_inc(logit_done, 1)
                    else:
                        dve.wait_ge(edge_logit, u + 1)
                        nc.vector.scalar_tensor_tensor(logit[:, s4, :], prod[:, 4 * G:8 * G], SLOPE, prod[:, 4 * G:8 * G],
                                                       ALU.mult, ALU.max).then_inc(logit_done, 1)

                def raise_a(v):
                    u, s, t, s4, t4 = v
                    dve.wait_ge(top_part, u + 1)
                    if not dot:
                        dve.wait_ge(q_done, up_to(u + 3))
                    nc.vector.tensor_scalar(absent[:], ps_top[:, 4:5], BIG, -BIG, ALU.mult, ALU.add).then_inc(absent_done, 1)

                def raise_b(v, kept):
                    u, s, t, s4, t4 = v
                    dve.wait_ge(absent_done, u + 1)
                    if known(u, 1):
                        dve.wait_ge(top_kept, u)
                    nc.vector.scalar_tensor_tensor(top[:], ps_top[:, 0:4], absent[:, 0:1], kept, ALU.add, ALU.max).then_inc(top_done, 1)

                def raise_c(v, kept):
                    u, s, t, s4, t4 = v
                    dve.wait_ge(top_done, u + 1)
                    nc.vector.tensor_copy(top_hi[:], top[:]).then_inc(top_high, 1)
                    nc.vector.tensor_tensor(drop[:, s % 2, :], kept, top[:], ALU.subtract).then_inc(drop_done, 1)

                def raise_d(v, kept):
                    u, s, t, s4, t4 = v
                    dve.wait_ge(top_high, u + 1)
                    nc.vector.tensor_tensor(top_lo[:], top[:], top_hi[:], ALU.subtract).then_inc(top_split, 1)
                    dve.wait_ge(drop_done, u + 1)
                    nc.vector.tensor_scalar(kept, top[:], 1.0, None, ALU.mult).then_inc(top_kept, 1)

                def gap_a(v):
                    u, s, t, s4, t4 = v
                    dve.wait_ge(ref_done, u + 1)
                    nc.vector.tensor_tensor(gap[:], logit[:, s4, :], ps_ref[:, 0:4 * G], ALU.subtract).then_inc(gap_part, 1)

                def gap_b(v):
                    u, s, t, s4, t4 = v
                    if softmax:
                        dve.wait_ge(gap_part, u + 1)
                        nc.vector.tensor_scalar(gap[:], gap[:], 60.0, None, ALU.min).then_inc(gap_done, 1)
                    else:
                        dve.wait_ge(logit_done, u + 1)
                        nc.vector.tensor_scalar(gap[:], logit[:, s4, :], -5.0, 5.0, ALU.max, ALU.min).then_inc(gap_done, 1)

                def fade_sums(v, blk):
                    u, s, t, s4, t4 = v
                    dve.wait_ge(fade_done, u + 1)
                    if known(u, 1):
                        dve.wait_ge(acc_done, u)
                    nc.vector.tensor_tensor(blk.rearrange("p (h w) -> p h w", w=hw), blk.rearrange("p (h w) -> p h w", w=hw),
                                            bcast(fade[:, s % 2, :], [P, heads, hw]), ALU.mult).then_inc(faded, 1)

                def add_sums(v, blk):
                    u, s, t, s4, t4 = v
                    if softmax:
                        dve.wait_ge(faded, u + 1)
                    elif known(u, 1):
                        dve.wait_ge(acc_done, u)
                    dve.wait_ge(sum_done, u + 1)
                    nc.vector.tensor_tensor(blk, blk, ps_sum[:, 0:aw], ALU.add).then_inc(acc_done, 1)

                def weigh(v):
                    u, s, t, s4, t4 = v
                    dve.wait_ge(weight_done, u + 1)
                    w = s % 2
                    vals = (rows[:, s, :, D:2 * D].rearrange("p g (h d) -> p g h d", d=hd) if dot
                            else rows[:, s].rearrange("p g (h w) -> p g h w", w=hw)[:, :, :, 0:hd])
                    nc.vector.tensor_tensor(wv4[:, w, :, :, 0:hd], vals, bcast(wv4[:, w, :, :, hd], [P, G, heads, hd]),
                                            ALU.mult).then_inc(wv_done, 1)

                def digits(v):
                    u, s, t, s4, t4 = v
                    if known(u, 2):
                        dve.wait_ge(hist_done, u)
                    elif u == 0:
                        dve.wait_ge(hist_done, 1)
                    for hot, digit, n in ((lo_hot, "src_lo", P), (hi_hot, "src_hi", NT)):
                        ins = nc.vector.tensor_tensor(hot[:, s % 2], c["iota_bf"][:, 0:n].unsqueeze(1).broadcast_to([P, G, n]),
                                                      bcast(res[digit][:, bass.ds(u * G, G)], [P, G, n]), ALU.is_equal)
                    ins.then_inc(hot_done, 1)

                blocks = {}

                def body(i, k, it):
                    after, now, before, earlier = (at(i, k, it, d) for d in (1, 0, -1, -2))
                    if softmax and now:
                        running_max(now)
                    if weighted and earlier:
                        weigh(earlier)
                    if k == 0:
                        blocks.clear()
                    for d, v in ((-1, before), (-2, earlier)):
                        if v and k + d not in blocks:
                            blocks[k + d] = block_of(dve, v[0])
                    if softmax and before:
                        kept = res["top"][:, bass.ds(blocks[k - 1] * 4, 4)]
                    if earlier:
                        blk = acc[:, bass.ds(blocks[k - 2] * aw, aw)]
                    if softmax and before:
                        raise_a(before)
                    if softmax and earlier:
                        fade_sums(earlier, blk)
                    if softmax and before:
                        raise_b(before, kept)
                    if weighted and after:
                        logits_a(after)
                    if softmax and now:
                        ends_a(now)
                    if softmax and before:
                        raise_c(before, kept)
                    if weighted and after:
                        logits_a2(after)
                    if softmax and now:
                        ends_b(now)
                    if weighted and after:
                        logits_b(after)
                    if softmax and before:
                        raise_d(before, kept)
                    if softmax and now:
                        ends_c(now)
                    if hist is not None and after:
                        digits(after)
                    if earlier:
                        add_sums(earlier, blk)
                    if softmax and before:
                        gap_a(before)
                    if weighted and before:
                        gap_b(before)
                visits(dve, body, 1)
                if hist is not None:
                    dve.wait_ge(hist_done, NV + 1)
                    nc.vector.tensor_copy(hist, ps_hist[:, 0:NT]).then_inc(one, 1)


class TurnedRows:

    def __init__(self, p, nc, c, x, typed=None, tag=""):
        self.nc, self.c, self.x, self.typed = nc, c, x, typed
        self.n = T if typed is not None else 1
        self.staged_rows = p.sb(tag + "staged_rows", [P, 2, self.n, D])
        self.rows = p.sb(tag + "turned_rows", [P, 2, self.n, P])
        self.ps = [p.ps(f"{tag}ps_turned{k}", [P, T, P]) for k in range(2)]
        self.staged, self.turned, self.copied, self.made = (
            p.sem(tag + n) for n in ("staged", "turned", "copied", "made"))

    def stage(self, pool, t, s):
        if known(t, 2):
            pool.wait_ge(self.turned, t - 1)
        tile = self.x[:, bass.ds(t, 1), :]
        if self.typed is None:
            self.nc.gpsimd.tensor_copy(self.staged_rows[:, s], tile).then_inc(self.staged, 1)
        else:
            shape = [P, T, D]
            kinds = self.typed[:, bass.ds(t, 1), :].rearrange("p t y -> p (t y)")
            self.nc.gpsimd.tensor_tensor(self.staged_rows[:, s], tile.broadcast_to(shape), bcast(kinds, shape),
                                         ALU.mult).then_inc(self.staged, 1)

    def ahead(self, step, eng, t, s):
        if isinstance(t, int) and t == 0:
            step(eng, 0, 0)
        if not isinstance(t, int) or t < NT - 1:
            step(eng, t + 1, 1 - s)

    def turn(self, pe, t, s):
        self.ahead(self.turn_tile, pe, t, s)

    def copy(self, act, t, s):
        self.ahead(self.copy_tile, act, t, s)

    def turn_tile(self, pe, t, s):
        pe.wait_ge(self.staged, t + 1)
        if known(t, 2):
            pe.wait_ge(self.copied, t - 1)
        for y in range(self.n):
            mm = self.nc.tensor.transpose(self.ps[s][:, y, :], self.staged_rows[:, s, y, :], self.c["ident"])
        mm.then_inc(self.turned, 1)

    def copy_tile(self, act, t, s):
        act.wait_ge(self.turned, t + 1)
        if known(t, 2):
            act.wait_ge(self.made, t - 1)
        self.nc.scalar.activation(self.rows[:, s], self.ps[s][:, 0:self.n, :], ACT.Copy).then_inc(self.copied, 1)


def norm_phase(nc, name, x, out, square, **how):
    with phase(nc, name) as p:
        ln = LayerNorm(p, x, out, square, **how)
        with nc.Block() as block:
            @block.vector
            def _(dve):
                ln.vector(nc, dve)

            @block.scalar
            def _(act):
                ln.scalar(nc, act)


def tile(x, t):
    return x[:, bass.ds(t, 1), :].rearrange("p t d -> p (t d)")


def row_of(ap):
    return ap.rearrange("(o d) -> o d", o=1).broadcast_to([P, ap.shape[0]])


def typed_tables(nc, c, w, h, typed, q, dram):
    with phase(nc, "l0pre") as p:
        wkv, wqp = p.sb("wkv", [P, T, 2, D]), p.sb("wqp", [P, T, 2, D])
        rel = p.sb("rel", [P, 2, R, D])
        pri = p.sb("pri", [P, 4, R])
        kv_t = p.sb("kv_t", [P, 2, 2, P])
        pre = p.sb("pre", [P, 2, D])
        out = p.sb("out", [P, 2, R, 2, D])
        tr = TurnedRows(p, nc, c, h, typed)
        ps_kv, ps_qp = p.ps("ps_kv", [P, 2, 256]), p.ps("ps_qp", [P, 2, 256])
        ps_rel = [p.ps(f"ps_rel{j}", [P, 4, D]) for j in range(4)]
        loaded, zeroed, scaled, rel_in, steps, kv_made, kv_copied, rel_made, rel_k, rel_v, q_taken, pre_taken = (
            p.sem(n) for n in ("loaded", "zeroed", "scaled", "rel_in", "steps", "kv_made", "kv_copied", "rel_made",
                               "rel_k", "rel_v", "q_taken", "pre_taken"))
        stored = [p.sem("stored0"), p.sem("stored1")]

        with nc.Block() as block:
            @block.sync
            def _(sp):
                for i, name in enumerate(("L0_gnn_W_k", "L0_gnn_W_v")):
                    sp.dma_start(wkv[:, :, i, :], w[name].rearrange("t i o -> i t o")).then_inc(loaded, 16)
                for i, name in enumerate(("L0_gnn_W_q", "L0_gnn_W_pre")):
                    sp.dma_start(wqp[:, :, i, :], w[name].rearrange("t i o -> i t o")).then_inc(loaded, 16)
                sp.dma_start(pri[:].rearrange("p h r -> p (h r)"), row_of(w["L0_gnn_rel_pri"].rearrange("h r -> (h r)"))).then_inc(loaded, 16)
                sp.wait_ge(zeroed, 1)
                for hh in range(4):
                    for i, name in enumerate(("L0_gnn_rel_att", "L0_gnn_rel_msg")):
                        sp.dma_start(rel[32 * hh:32 * hh + 32, i, :, 32 * hh:32 * hh + 32],
                                     w[name][hh].rearrange("r d f -> d r f")).then_inc(rel_in, 16)

                def store(t, s, turn):
                    sp.wait_ge(rel_k, t + 1)
                    sp.wait_ge(rel_v, t + 1)
                    sp.dma_start(dram["kv_typed"][bass.ds(t, 1)].rearrange("t p f -> (t p) f"),
                                 out[:, s].rearrange("p r k d -> p (r k d)")).then_inc(stored[s], 16)
                    sp.wait_ge(pre_taken, t + 1)
                    sp.dma_start(tile(dram["pre"], t), pre[:, s]).then_inc(stored[s], 16)
                node_tiles(sp, store)
                sp.wait_ge(stored[0], 32 * (NT // 2 + 1))
                sp.wait_ge(stored[1], 32 * (NT // 2))

            @block.gpsimd
            def _(pool):
                node_tiles(pool, lambda t, s, turn: tr.stage(pool, t, s))

            @block.tensor
            def _(pe):
                pe.wait_ge(loaded, 80)
                pe.wait_ge(scaled, 1)

                def body(t, s, turn):
                    tr.turn(pe, t, s)
                    pe.wait_ge(tr.copied, t + 1)
                    if known(t, 1):
                        pe.wait_ge(kv_copied, t)
                        pe.wait_ge(q_taken, t)
                        pe.wait_ge(pre_taken, t)
                    for i in range(2):
                        for y in range(T):
                            mm = nc.tensor.matmul(ps_kv[:, i, 0:P], wkv[:, y, i, :], tr.rows[:, s, y, :], start=y == 0, stop=y == T - 1)
                    mm.then_inc(kv_made, 1)
                    for y in range(T):
                        mm = nc.tensor.matmul(ps_qp[:, 0, :], tr.rows[:, s, y, :], wqp[:, y, :, :], start=y == 0, stop=y == T - 1)
                    mm.then_inc(tr.made, 1)
                    pe.wait_ge(kv_copied, t + 1)
                    if known(t, 1):
                        pe.wait_ge(rel_k, t)
                        pe.wait_ge(rel_v, t)
                    for i in range(2):
                        for half in range(2):
                            mm = nc.tensor.matmul(ps_rel[2 * i + half][:], kv_t[:, s, i, :], rel[:, i, 4 * half:4 * half + 4, :],
                                                  start=True, stop=True)
                    mm.then_inc(rel_made, 1)
                node_tiles(pe, body)

            @block.scalar
            def _(act):
                def body(t, s, turn):
                    tr.copy(act, t, s)
                    act.wait_ge(kv_made, t + 1)
                    if known(t, 2):
                        act.wait_ge(rel_made, t - 1)
                    nc.scalar.activation(kv_t[:, s], ps_kv[:, :, 0:P], ACT.Copy).then_inc(kv_copied, 1)
                    act.wait_ge(tr.made, t + 1)
                    if known(t, 2):
                        act.wait_ge(stored[s], turn * 32)
                    nc.scalar.activation(pre[:, s], ps_qp[:, 0, D:2 * D], ACT.Copy).then_inc(pre_taken, 1)
                    nc.scalar.activation(tile(q, t), ps_qp[:, 0, 0:D], ACT.Copy).then_inc(q_taken, 1)
                    act.wait_ge(rel_made, t + 1)
                    for half in range(2):
                        ins = nc.scalar.activation(out[:, s, 4 * half:4 * half + 4, 1, :], ps_rel[2 + half][:], ACT.Copy)
                    ins.then_inc(rel_v, 1)
                node_tiles(act, body)

            @block.vector
            def _(dve):
                link = Chain(dve, steps)
                nc.vector.memset(rel[:], 0.0).then_inc(zeroed, 1)
                dve.wait_ge(loaded, 80)
                link(nc.vector.tensor_scalar(pri[:], pri[:], float(1.0 / np.sqrt(32.0)), None, ALU.mult))
                dve.wait_ge(rel_in, 128)
                for r in range(R):
                    block_r = rel[:, 0, r, :].rearrange("p (h f) -> p h f", f=32)
                    ins = nc.vector.tensor_tensor(block_r, block_r, bcast(pri[:, :, r], [P, 4, 32]), ALU.mult)
                ins.then_inc(scaled, 1)

                def body(t, s, turn):
                    dve.wait_ge(rel_made, t + 1)
                    if known(t, 2):
                        dve.wait_ge(stored[s], turn * 32)
                    for half in range(2):
                        ins = nc.vector.tensor_copy(out[:, s, 4 * half:4 * half + 4, 0, :], ps_rel[half][:])
                    ins.then_inc(rel_k, 1)
                node_tiles(dve, body)


def typed_output(nc, c, w, x, h, typed, acc, mix, dram):
    with phase(nc, "l0post") as p:
        wa = p.sb("wa", [P, T, D])
        skip = p.sb("skip", [P, T])
        alpha, rest = p.sb("alpha", [P, NT]), p.sb("rest", [P, NT])
        picked = p.sb("picked", [P, NT, T])
        tr = TurnedRows(p, nc, c, mix, typed)
        ps_out = p.ps("ps_out", [P, 2, 512])
        loaded, steps, negated, gated, mixed, done = (p.sem(n) for n in ("loaded", "steps", "negated", "gated", "mixed", "done"))
        acc4 = acc.rearrange("p (t h w) -> p t h w", h=4, w=33)
        with nc.Block() as block:
            @block.sync
            def _(sp):
                sp.dma_start(wa[:], w["L0_gnn_W_a"].rearrange("t i o -> i t o")).then_inc(loaded, 16)
                sp.dma_start(skip[:], row_of(w["L0_gnn_skip"])).then_inc(loaded, 16)
                sp.dma_start(mix, dram["pre"]).then_inc(loaded, 16)

            @block.scalar
            def _(act):
                act.wait_ge(negated, 1)
                nc.scalar.activation(skip[:], skip[:], ACT.Exp, scale=-1.0).then_inc(gated, 1)
                node_tiles(act, lambda t, s, turn: tr.copy(act, t, s))

            @block.gpsimd
            def _(pool):
                pool.wait_ge(mixed, 1)
                node_tiles(pool, lambda t, s, turn: tr.stage(pool, t, s))

            @block.tensor
            def _(pe):
                def body(t, s, turn):
                    tr.turn(pe, t, s)
                    pe.wait_ge(tr.copied, t + 1)
                    if known(t, 2):
                        pe.wait_ge(done, t - 1)
                    for y in range(T):
                        mm = nc.tensor.matmul(ps_out[:, s, 0:D], tr.rows[:, s, y, :], wa[:, y, :], start=y == 0, stop=y == T - 1)
                    mm.then_inc(tr.made, 1)
                node_tiles(pe, body)

            @block.vector
            def _(dve):
                link = Chain(dve, steps)
                z = acc4[:, :, :, 32]
                link(nc.vector.tensor_scalar(z, z, 1e-30, None, ALU.max))
                link(nc.vector.reciprocal(z, z))
                dve.wait_ge(loaded, 48)
                nc.vector.tensor_copy(picked[:], typed).then_inc(negated, 1)
                link(nc.vector.tensor_tensor(acc4[:, :, :, 0:32], acc4[:, :, :, 0:32], bcast(z, [P, NT, 4, 32]), ALU.mult))
                link(nc.vector.tensor_scalar(mix, mix, 1.0 - LAM, None, ALU.mult))
                link(nc.vector.tensor_scalar(acc4[:, :, :, 0:32], acc4[:, :, :, 0:32], LAM, None, ALU.mult))
                nc.vector.tensor_tensor(mix.rearrange("p t (h f) -> p t h f", f=32), mix.rearrange("p t (h f) -> p t h f", f=32),
                                        acc4[:, :, :, 0:32], ALU.add).then_inc(mixed, 1)
                dve.wait_ge(gated, 1)
                link(nc.vector.tensor_scalar(skip[:], skip[:], 1.0, None, ALU.add))
                link(nc.vector.reciprocal(skip[:], skip[:]))
                link(nc.vector.tensor_tensor(picked[:], typed, skip[:].unsqueeze(1).broadcast_to([P, NT, T]), ALU.mult))
                link(nc.vector.reduce_sum(alpha[:], picked[:], AX.X))
                link(nc.vector.tensor_scalar(rest[:], alpha[:], -1.0, 1.0, ALU.mult, ALU.add))
                link(nc.vector.tensor_tensor(h, h, bcast(rest[:], [P, NT, D]), ALU.mult))
                link(nc.vector.tensor_tensor(x, x, h, ALU.add))

                def body(t, s, turn):
                    dve.wait_ge(tr.made, t + 1)
                    nc.vector.scalar_tensor_tensor(tile(x, t), ps_out[:, s, 0:D], alpha[:, bass.ds(t, 1)], tile(x, t),
                                                   ALU.mult, ALU.add).then_inc(done, 1)
                node_tiles(dve, body)


def gat_tables(nc, c, w, g, acc, top, ad, dram):
    with phase(nc, "l1pre") as p:
        wt = p.sb("wt", [P, D])
        att = p.sb("att", [P, 2, D])
        part = p.sb("part", [P, NT, D])
        a_sum, a_self, t_hi = p.sb("a_sum", [P, NT, 4]), p.sb("a_self", [P, NT, 4]), p.sb("t_hi", [P, NT, 4], BF16)
        t_lo = p.sb("t_lo", [P, NT, 4], BF16)
        self_gap, self_exp = p.sem("self_gap"), p.sem("self_exp")
        tr = TurnedRows(p, nc, c, g)
        ps_out = p.ps("ps_out", [P, 2, 512])
        loaded, steps, done, table_ready, table_out = (p.sem(n) for n in ("loaded", "steps", "done", "table_ready", "table_out"))
        acc4 = acc.rearrange("p (t h w) -> p t h w", h=4, w=33)
        with nc.Block() as block:
            @block.sync
            def _(sp):
                sp.dma_start(wt[:], w["L1_gnn_W"]).then_inc(loaded, 16)
                sp.dma_start(att[:, 0, :], row_of(w["L1_gnn_att_src"].rearrange("h c -> (h c)"))).then_inc(loaded, 16)
                sp.dma_start(att[:, 1, :], row_of(w["L1_gnn_att_dst"].rearrange("h c -> (h c)"))).then_inc(loaded, 16)
                sp.wait_ge(table_ready, 1)
                sp.dma_start(dram["gat"].rearrange("(t p) f -> p t f", p=P), acc.rearrange("p (t f) -> p t f", t=NT)).then_inc(table_out, 16)
                sp.wait_ge(table_out, 16)

            @block.scalar
            def _(act):
                node_tiles(act, lambda t, s, turn: tr.copy(act, t, s))
                act.wait_ge(self_gap, 1)
                nc.scalar.activation(a_self[:], a_self[:], ACT.Exp).then_inc(self_exp, 1)

            @block.gpsimd
            def _(pool):
                node_tiles(pool, lambda t, s, turn: tr.stage(pool, t, s))

            @block.tensor
            def _(pe):
                pe.wait_ge(loaded, 48)

                def body(t, s, turn):
                    tr.turn(pe, t, s)
                    pe.wait_ge(tr.copied, t + 1)
                    if known(t, 2):
                        pe.wait_ge(done, t - 1)
                    nc.tensor.matmul(ps_out[:, s, 0:D], tr.rows[:, s, 0, :], wt[:], start=True, stop=True).then_inc(tr.made, 1)
                node_tiles(pe, body)

            @block.vector
            def _(dve):
                link = Chain(dve, steps)

                def body(t, s, turn):
                    dve.wait_ge(tr.made, t + 1)
                    nc.vector.tensor_scalar(acc[:, bass.ds(t * 132, 132)].rearrange("p (h w) -> p h w", w=33)[:, :, 0:32],
                                            ps_out[:, s, 0:D].rearrange("p (h f) -> p h f", f=32), 1.0, None, ALU.mult).then_inc(done, 1)
                node_tiles(dve, body)
                dve.wait_ge(done, NT)
                dve.wait_ge(loaded, 48)
                rows4 = part[:].rearrange("p t (h f) -> p t h f", f=32)
                for i, out in ((0, acc4[:, :, :, 32]), (1, a_sum[:])):
                    for hh in range(4):
                        ins = nc.vector.tensor_tensor(rows4[:, :, hh, :], acc4[:, :, hh, 0:32],
                                                      att[:, i, 32 * hh:32 * hh + 32].unsqueeze(1).broadcast_to([P, NT, 32]), ALU.mult)
                    link(ins)
                    link(nc.vector.reduce_sum(out, rows4, AX.X))
                top3 = top.rearrange("p (t h) -> p t h", h=4)
                link(nc.vector.tensor_tensor(a_self[:], acc4[:, :, :, 32], a_sum[:], ALU.add))
                nc.vector.scalar_tensor_tensor(a_self[:], a_self[:], SLOPE, a_self[:], ALU.mult, ALU.max).then_inc(table_ready, 1)
                ad4 = ad.rearrange("p (t k h) -> p t k h", k=3, h=4)
                for k in range(3):
                    link(nc.vector.tensor_copy(ad4[:, :, k, :], a_sum[:]))
                    if k < 2:
                        link(nc.vector.tensor_tensor(a_sum[:], a_sum[:], ad4[:, :, k, :], ALU.subtract))
                dve.wait_ge(table_ready, 1)
                link(nc.vector.tensor_copy(t_hi[:], a_self[:]))
                link(nc.vector.tensor_tensor(t_lo[:], a_self[:], t_hi[:], ALU.subtract))
                link(nc.vector.tensor_tensor(top3, t_hi[:], t_lo[:], ALU.add))
                nc.vector.tensor_tensor(a_self[:], a_self[:], top3, ALU.subtract).then_inc(self_gap, 1)
                dve.wait_ge(table_out, 16)
                dve.wait_ge(self_exp, 1)
                link(nc.vector.tensor_copy(acc4[:, :, :, 32], a_self[:]))
                link(nc.vector.tensor_tensor(acc4[:, :, :, 0:32], acc4[:, :, :, 0:32], bcast(a_self[:], [P, NT, 4, 32]), ALU.mult))


def gat_output(nc, c, w, h, acc, g):
    with phase(nc, "l1post") as p:
        bias = p.sb("bias", [P, D])
        loaded, steps = p.sem("loaded"), p.sem("steps")
        acc4 = acc.rearrange("p (t h w) -> p t h w", h=4, w=33)
        with nc.Block() as block:
            @block.sync
            def _(sp):
                sp.dma_start(bias[:], row_of(w["L1_gnn_gat_b"])).then_inc(loaded, 16)

            @block.vector
            def _(dve):
                link = Chain(dve, steps)
                z = acc4[:, :, :, 32]
                link(nc.vector.reciprocal(z, z))
                link(nc.vector.tensor_tensor(g.rearrange("p t (h f) -> p t h f", f=32), acc4[:, :, :, 0:32], bcast(z, [P, NT, 4, 32]), ALU.mult))
                dve.wait_ge(loaded, 16)
                link(nc.vector.tensor_tensor(g, g, bias[:].unsqueeze(1).broadcast_to([P, NT, D]), ALU.add))
                link(nc.vector.tensor_tensor(g, g, h, ALU.add))


def feed_forward(nc, name, c, w1, b1, w2, b2, func, x, into):
    with phase(nc, name) as p:
        w1s, w2s = p.sb("w1s", [P, 2 * D]), p.sb("w2s", [P, 2, D])
        b1s, b2s = p.sb("b1s", [P, 2]), p.sb("b2s", [P, D])
        hidden = p.sb("hidden", [P, 2, 2, P])
        tr = TurnedRows(p, nc, c, x)
        ps_hid, ps_out = p.ps("ps_hid", [P, 2, 2, 256]), p.ps("ps_out", [P, 2, 512])
        loaded, hid_done, out_made, done, biased = (p.sem(n) for n in ("loaded", "hid_done", "out_made", "done", "biased"))
        with nc.Block() as block:
            @block.sync
            def _(sp):
                sp.dma_start(w1s[:], w1).then_inc(loaded, 16)
                sp.dma_start(w2s[:], w2.rearrange("(c k) o -> k c o", c=2)).then_inc(loaded, 16)
                sp.dma_start(b1s[:], b1).then_inc(loaded, 16)
                sp.dma_start(b2s[:], row_of(b2)).then_inc(loaded, 16)

            @block.gpsimd
            def _(pool):
                node_tiles(pool, lambda t, s, turn: tr.stage(pool, t, s))

            @block.tensor
            def _(pe):
                pe.wait_ge(loaded, 64)

                def body(t, s, turn):
                    tr.turn(pe, t, s)
                    pe.wait_ge(tr.copied, t + 1)
                    if known(t, 2):
                        pe.wait_ge(hid_done, t - 1)
                    for j in range(2):
                        mm = nc.tensor.matmul(ps_hid[:, s, j, 0:P], w1s[:, j * D:(j + 1) * D], tr.rows[:, s, 0, :], start=True, stop=True)
                    mm.then_inc(tr.made, 1)
                    if known(t, 1):
                        second(t - 1, 1 - s)

                def second(t, s):
                    pe.wait_ge(hid_done, t + 1)
                    if not isinstance(t, int) or t >= 1:
                        pe.wait_ge(done, t)
                    for j in range(2):
                        mm = nc.tensor.matmul(ps_out[:, s, 0:D], hidden[:, s, j, :], w2s[:, j, :], start=j == 0, stop=j == 1)
                    mm.then_inc(out_made, 1)
                node_tiles(pe, body)
                second(NT - 1, 0)

            @block.scalar
            def _(act):
                act.wait_ge(loaded, 64)

                def body(t, s, turn):
                    tr.copy(act, t, s)
                    act.wait_ge(tr.made, t + 1)
                    if known(t, 2):
                        act.wait_ge(out_made, t - 1)
                    for j in range(2):
                        ins = nc.scalar.activation(hidden[:, s, j, :], ps_hid[:, s, j, 0:P], func, bias=b1s[:, j:j + 1])
                    ins.then_inc(hid_done, 1)
                node_tiles(act, body)

            @block.vector
            def _(dve):
                dve.wait_ge(loaded, 64)
                nc.vector.tensor_tensor(into, into, b2s[:].unsqueeze(1).broadcast_to([P, NT, D]), ALU.add).then_inc(biased, 1)
                dve.wait_ge(biased, 1)

                def body(t, s, turn):
                    dve.wait_ge(out_made, t + 1)
                    nc.vector.tensor_tensor(tile(into, t), tile(into, t), ps_out[:, s, 0:D], ALU.add).then_inc(done, 1)
                node_tiles(dve, body)


def conv_table(nc, h, out_deg, part, dram):
    with phase(nc, "l2pre") as p:
        steps, clipped, rooted, ready, stored = (p.sem(n) for n in ("steps", "clipped", "rooted", "ready", "stored"))
        with nc.Block() as block:
            @block.scalar
            def _(act):
                act.wait_ge(clipped, 1)
                nc.scalar.activation(out_deg, out_deg, ACT.Sqrt).then_inc(rooted, 1)

            @block.vector
            def _(dve):
                link = Chain(dve, steps)
                nc.vector.tensor_scalar(out_deg, out_deg, 1.0, None, ALU.max).then_inc(clipped, 1)
                dve.wait_ge(rooted, 1)
                link(nc.vector.reciprocal(out_deg, out_deg))
                nc.vector.memset(part[:, :, D:D + 1], 1.0)
                nc.vector.tensor_tensor(part[:, :, 0:D], h, bcast(out_deg, [P, NT, D]), ALU.mult).then_inc(ready, 1)

            @block.sync
            def _(sp):
                sp.wait_ge(ready, 1)
                sp.dma_start(dram["conv"].rearrange("(t p) f -> p t f", p=P), part).then_inc(stored, 16)
                sp.wait_ge(stored, 16)


def conv_output(nc, c, w, x, acc, g):
    with phase(nc, "l2post") as p:
        wt, bias, deg = p.sb("wt", [P, D]), p.sb("bias", [P, D]), p.sb("deg", [P, NT])
        tr = TurnedRows(p, nc, c, acc[:, :, 0:D])
        ps_out = p.ps("ps_out", [P, 2, 512])
        loaded, steps, clipped, rooted, done = (p.sem(n) for n in ("loaded", "steps", "clipped", "rooted", "done"))
        with nc.Block() as block:
            @block.sync
            def _(sp):
                sp.dma_start(wt[:], w["L2_gnn_weight"]).then_inc(loaded, 16)
                sp.dma_start(bias[:], row_of(w["L2_gnn_bias"])).then_inc(loaded, 16)

            @block.scalar
            def _(act):
                act.wait_ge(clipped, 1)
                nc.scalar.activation(deg[:], deg[:], ACT.Sqrt).then_inc(rooted, 1)
                node_tiles(act, lambda t, s, turn: tr.copy(act, t, s))

            @block.gpsimd
            def _(pool):
                node_tiles(pool, lambda t, s, turn: tr.stage(pool, t, s))

            @block.tensor
            def _(pe):
                pe.wait_ge(loaded, 32)

                def body(t, s, turn):
                    tr.turn(pe, t, s)
                    pe.wait_ge(tr.copied, t + 1)
                    if known(t, 2):
                        pe.wait_ge(done, t - 1)
                    nc.tensor.matmul(ps_out[:, s, 0:D], tr.rows[:, s, 0, :], wt[:], start=True, stop=True).then_inc(tr.made, 1)
                node_tiles(pe, body)

            @block.vector
            def _(dve):
                link = Chain(dve, steps)
                nc.vector.tensor_scalar(deg[:], acc[:, :, D], 1.0, None, ALU.max).then_inc(clipped, 1)
                dve.wait_ge(rooted, 1)
                link(nc.vector.reciprocal(deg[:], deg[:]))
                dve.wait_ge(loaded, 32)

                def body(t, s, turn):
                    dve.wait_ge(tr.made, t + 1)
                    nc.vector.scalar_tensor_tensor(tile(g, t), ps_out[:, s, 0:D], deg[:, bass.ds(t, 1)], bias[:],
                                                   ALU.mult, ALU.add).then_inc(done, 1)
                node_tiles(dve, body)
                dve.wait_ge(done, NT)
                link(nc.vector.tensor_scalar(g, g, 0.0, None, ALU.max))
                link(nc.vector.tensor_tensor(x, x, g, ALU.add))


def attention_tables(nc, c, w, h, q, dram):
    with phase(nc, "l3pre") as p:
        wt = p.sb("wt", [P, 3, D])
        kv = p.sb("kv", [P, 2, 2 * D])
        tr = TurnedRows(p, nc, c, h)
        ps_out = [p.ps("ps_out0", [P, 512]), p.ps("ps_out1", [P, 512])]
        loaded, q_taken, kv_taken = (p.sem(n) for n in ("loaded", "q_taken", "kv_taken"))
        stored = [p.sem("stored0"), p.sem("stored1")]
        with nc.Block() as block:
            @block.sync
            def _(sp):
                for i, name in enumerate(("L3_gnn_Wq", "L3_gnn_Wk", "L3_gnn_Wv")):
                    sp.dma_start(wt[:, i, :], w[name]).then_inc(loaded, 16)

                def store(t, s, turn):
                    sp.wait_ge(kv_taken, t + 1)
                    sp.dma_start(dram["kv"][bass.ds(t, 1)].rearrange("t p f -> (t p) f"), kv[:, s]).then_inc(stored[s], 16)
                node_tiles(sp, store)
                sp.wait_ge(stored[0], 16 * (NT // 2 + 1))
                sp.wait_ge(stored[1], 16 * (NT // 2))

            @block.scalar
            def _(act):
                def body(t, s, turn):
                    tr.copy(act, t, s)
                    act.wait_ge(kv_taken, t + 1)
                    nc.scalar.activation(tile(q, t), ps_out[s][:, 0:D], ACT.Copy, scale=0.25).then_inc(q_taken, 1)
                node_tiles(act, body)

            @block.gpsimd
            def _(pool):
                node_tiles(pool, lambda t, s, turn: tr.stage(pool, t, s))

            @block.tensor
            def _(pe):
                pe.wait_ge(loaded, 48)

                def body(t, s, turn):
                    tr.turn(pe, t, s)
                    pe.wait_ge(tr.copied, t + 1)
                    if known(t, 2):
                        pe.wait_ge(q_taken, t - 1)
                        pe.wait_ge(kv_taken, t - 1)
                    nc.tensor.matmul(ps_out[s][:, 0:3 * D], tr.rows[:, s, 0, :], wt[:], start=True, stop=True).then_inc(tr.made, 1)
                node_tiles(pe, body)

            @block.vector
            def _(dve):
                def body(t, s, turn):
                    dve.wait_ge(tr.made, t + 1)
                    if known(t, 2):
                        dve.wait_ge(stored[s], turn * 16)
                    nc.vector.tensor_copy(kv[:, s], ps_out[s][:, D:3 * D]).then_inc(kv_taken, 1)
                node_tiles(dve, body)


def attention_output(nc, c, w, h, acc, g, out):
    with phase(nc, "l3post") as p:
        wt, bias = p.sb("wt", [P, D]), p.sb("bias", [P, D])
        tr = TurnedRows(p, nc, c, g)
        ps_out = p.ps("ps_out", [P, 2, 512])
        loaded, steps, mixed, done = (p.sem(n) for n in ("loaded", "steps", "mixed", "done"))
        acc4 = acc.rearrange("p (t h w) -> p t h w", h=8, w=17)
        with nc.Block() as block:
            @block.sync
            def _(sp):
                sp.dma_start(wt[:], w["L3_gnn_Wo"]).then_inc(loaded, 16)
                sp.dma_start(bias[:], row_of(w["L3_gnn_bo"])).then_inc(loaded, 16)

            @block.scalar
            def _(act):
                node_tiles(act, lambda t, s, turn: tr.copy(act, t, s))

            @block.gpsimd
            def _(pool):
                pool.wait_ge(mixed, 1)
                node_tiles(pool, lambda t, s, turn: tr.stage(pool, t, s))

            @block.tensor
            def _(pe):
                pe.wait_ge(loaded, 32)

                def body(t, s, turn):
                    tr.turn(pe, t, s)
                    pe.wait_ge(tr.copied, t + 1)
                    if known(t, 2):
                        pe.wait_ge(done, t - 1)
                    nc.tensor.matmul(ps_out[:, s, 0:D], tr.rows[:, s, 0, :], wt[:], start=True, stop=True).then_inc(tr.made, 1)
                node_tiles(pe, body)

            @block.vector
            def _(dve):
                link = Chain(dve, steps)
                z = acc4[:, :, :, 16]
                link(nc.vector.tensor_scalar(z, z, 1e-6, None, ALU.add))
                link(nc.vector.reciprocal(z, z))
                nc.vector.tensor_tensor(g.rearrange("p t (h f) -> p t h f", f=16), acc4[:, :, :, 0:16],
                                        bcast(z, [P, NT, 8, 16]), ALU.mult).then_inc(mixed, 1)
                dve.wait_ge(loaded, 32)
                link(nc.vector.tensor_tensor(out, h, bias[:].unsqueeze(1).broadcast_to([P, NT, D]), ALU.add))

                def body(t, s, turn):
                    dve.wait_ge(tr.made, t + 1)
                    nc.vector.tensor_tensor(tile(out, t), tile(out, t), ps_out[:, s, 0:D], ALU.add).then_inc(done, 1)
                node_tiles(dve, body)


def batch_norm(nc, name, c, weight, bias, x, square, add_to=None):
    with phase(nc, name) as p:
        wr, br, mean, scale = (p.sb(n, [P, D]) for n in ("wr", "br", "mean", "scale"))
        slab = p.sb("slab", [P, 2, D])
        ps_mean, ps_var = p.ps("ps_mean", [P, 512]), p.ps("ps_var", [P, 512])
        loaded, steps, mean_made, centred, squared, var_made, var_ready, rooted = (
            p.sem(n) for n in ("loaded", "steps", "mean_made", "centred", "squared", "var_made", "var_ready", "rooted"))

        def rows(ap):
            return ap.unsqueeze(1).broadcast_to([P, NT, D])

        with nc.Block() as block:
            @block.sync
            def _(sp):
                sp.dma_start(wr[:], row_of(weight)).then_inc(loaded, 16)
                sp.dma_start(br[:], row_of(bias)).then_inc(loaded, 16)

            @block.tensor
            def _(pe):
                def column_sums(ps, v):
                    nc.tensor.matmul(ps[:, 0:D], c["ones_last"], v[:, NT - 1, :], start=True, stop=False)
                    with pe.Fori(0, NT - 2) as t:
                        nc.tensor.matmul(ps[:, 0:D], c["ones"], tile(v, t), start=False, stop=False)
                    return nc.tensor.matmul(ps[:, 0:D], c["ones"], v[:, NT - 2, :], start=False, stop=True)
                column_sums(ps_mean, x).then_inc(mean_made, 1)
                pe.wait_ge(squared, 1)
                column_sums(ps_var, square).then_inc(var_made, 1)

            @block.scalar
            def _(act):
                act.wait_ge(centred, 1)
                nc.scalar.activation(square, x, ACT.Square).then_inc(squared, 1)
                act.wait_ge(var_ready, 1)
                nc.scalar.activation(scale[:], scale[:], ACT.Sqrt).then_inc(rooted, 1)

            @block.vector
            def _(dve):
                link = Chain(dve, steps)
                dve.wait_ge(mean_made, 1)
                link(nc.vector.tensor_scalar(mean[:], ps_mean[:, 0:D], 1.0 / N, None, ALU.mult))
                nc.vector.tensor_tensor(x, x, rows(mean[:]), ALU.subtract).then_inc(centred, 1)
                dve.wait_ge(var_made, 1)
                nc.vector.tensor_scalar(scale[:], ps_var[:, 0:D], 1.0 / N, LN_EPS, ALU.mult, ALU.add).then_inc(var_ready, 1)
                dve.wait_ge(rooted, 1)
                link(nc.vector.reciprocal(scale[:], scale[:]))
                dve.wait_ge(loaded, 32)
                link(nc.vector.tensor_tensor(scale[:], scale[:], wr[:], ALU.mult))
                link(nc.vector.tensor_tensor(x, x, rows(scale[:]), ALU.mult))
                link(nc.vector.tensor_tensor(x, x, rows(br[:]), ALU.add))
                if add_to is not None:
                    link(nc.vector.tensor_tensor(add_to, add_to, x, ALU.add))


def graph_layers(nc, w, consts, out):
    dram = {
        "blocks": nc.dram_tensor("visit_blocks", (NV,), I32).ap(),
        "feat": nc.dram_tensor("visit_features", (NV, 5, GE), BF16).ap(),
        "idx_typed": nc.dram_tensor("visit_typed_sources", (P, NV, G), I32).ap(),
        "idx_src": nc.dram_tensor("visit_sources", (P, NV, G), I32).ap(),
        "last": nc.dram_tensor("visit_segment_ends", (P, NV, G), BF16).ap(),
        "flag": nc.dram_tensor("visit_flags", (NV, GE), BF16).ap(),
        "kv_typed": nc.dram_tensor("kv_typed", (NT, P, R * 2 * D), F32).ap(),
        "pre": nc.dram_tensor("pre_rows", (P, NT, D), F32).ap(),
        "gat": nc.dram_tensor("gat_rows", (NP, 132), F32).ap(),
        "conv": nc.dram_tensor("conv_rows", (NP, D + 1), F32).ap(),
        "kv": nc.dram_tensor("kv_rows", (NT, P, 2 * D), F32).ap(),
    }
    with ExitStack() as ctx:
        def sb(name, shape, dt=F32):
            return ctx.enter_context(nc.sbuf_tensor(name, shape, dt))

        x = sb("x", [P, NT, D])
        top, out_deg = sb("top", [P, NT * 4]), sb("out_deg", [P, NT])
        a_dst = sb("a_dst", [P, NT * 12], BF16)
        typed, kinds = sb("typed", [P, NT, T]), sb("kinds", [P, NT], I32)
        ident, ones, ones_last = sb("ident", [P, P]), sb("ones", [P, P]), sb("ones_last", [P, P])
        col_f, col_feat = sb("col_f", [5, P]), sb("col_feat", [5, P], BF16)
        iota_f, iota_bf = sb("iota_f", [P, P]), sb("iota_bf", [P, P], BF16)
        res = {
            "blocks": sb("block_row", [1, NV], I32), "top": top,
            "src_lo": sb("src_lo", [P, NV * G], BF16), "src_hi": sb("src_hi", [P, NV * G], BF16),
        }
        c = {"ident": ident[:], "col_feat": col_feat[:], "iota_bf": iota_bf[:], "ones": ones[:], "ones_last": ones_last[:],
             "visit_ids": consts["visit_ids"], "group_ids": consts["group_ids"]}

        with phase(nc, "load") as p:
            loaded, steps = p.sem("loaded"), p.sem("steps")
            with nc.Block() as block:
                @block.sync
                def _(sp):
                    sp.dma_start(x[:], w["x"]).then_inc(loaded, 16)
                    sp.dma_start(kinds[:], w["node_type_4"]).then_inc(loaded, 16)
                    sp.dma_start(ident[:], consts["ident"]).then_inc(loaded, 16)
                    sp.dma_start(col_f[:], consts["col_feat"]).then_inc(loaded, 16)
                    sp.dma_start(iota_f[:], consts["iota"].broadcast_to([P, P])).then_inc(loaded, 16)
                    sp.dma_start(ones_last[:], consts["ones_last"]).then_inc(loaded, 16)
                    sp.wait_ge(loaded, 96)

                @block.vector
                def _(dve):
                    link = Chain(dve, steps)
                    link(nc.vector.memset(ones[:], 1.0))
                    link(nc.vector.memset(top[:], -BIG))
                    dve.wait_ge(loaded, 96)
                    link(nc.vector.tensor_copy(col_feat[:], col_f[:]))
                    link(nc.vector.tensor_copy(iota_bf[:], iota_f[:]))
                    for y in range(T):
                        link(nc.vector.tensor_scalar(typed[:, :, y], kinds[:], float(y), None, ALU.is_equal))

        edge = {"ends": w["group_ends"], "dst": w["dst"], "src": w["src"], "et": w["edge_type_8"]}
        plan_visits(nc, c, edge, dram, res)

        h, q = sb("h", [P, NT, D]), sb("q", [P, NT, D])
        sums = sb("sums", [P, NT * 136])
        square = sums[:, 0:NT * D].rearrange("p (t d) -> p t d", d=D)

        def clear_sums():
            with phase(nc, "clear%d" % len(cleared)) as p:
                cleared.append(1)
                with nc.Block() as block:
                    @block.vector
                    def _(dve):
                        nc.vector.memset(sums[:], 0.0).then_inc(p.sem("zeroed"), 1)
        cleared = []

        norm_phase(nc, "ln0", x[:], h[:], square, relu=True)
        typed_tables(nc, c, w, h[:], typed[:], q[:], dram)
        clear_sums()
        q2 = q[:].rearrange("p t d -> p (t d)")
        edge_pass(nc, "edges0", c, dram, res, dram["kv_typed"].rearrange("t p (r f) -> (t p r) f", r=R), dram["idx_typed"],
                  2 * D, 4, True, True, sums[:, 0:NT * 132], q=q2)
        typed_output(nc, c, w, x[:], h[:], typed[:], sums[:, 0:NT * 132], q[:], dram)

        norm_phase(nc, "ln1", x[:], h[:], square, relu=True)
        for_rows(nc, "ln1g", w["L1_gnn_ln1_g"], w["L1_gnn_ln1_b"], h[:], q[:], square)
        gat_tables(nc, c, w, q[:], sums[:, 0:NT * 132], top[:], a_dst[:], dram)
        edge_pass(nc, "edges1", c, dram, res, dram["gat"], dram["idx_src"], 132, 4, False, True, sums[:, 0:NT * 132],
                  q=a_dst[:], hist=out_deg[:])
        gat_output(nc, c, w, h[:], sums[:, 0:NT * 132], q[:])
        for_rows(nc, "ln2g", w["L1_gnn_ln2_g"], w["L1_gnn_ln2_b"], q[:], h[:], square, add=x[:])
        feed_forward(nc, "ffn1", c, w["L1_gnn_w1"], w["L1_gnn_b1"], w["L1_gnn_w2"], w["L1_gnn_b2"], ACT.Gelu, h[:], x[:])

        norm_phase(nc, "ln2", x[:], h[:], square, relu=True)
        conv = sums[:, 0:NT * (D + 1)]
        conv3 = conv.rearrange("p (t f) -> p t f", t=NT)
        conv_table(nc, h[:], out_deg[:], conv3, dram)
        clear_sums()
        edge_pass(nc, "edges2", c, dram, res, dram["conv"], dram["idx_src"], D + 1, 0, False, False, conv)
        conv_output(nc, c, w, x[:], conv3, q[:])

        norm_phase(nc, "ln3", x[:], h[:], square, relu=True)
        attention_tables(nc, c, w, h[:], q[:], dram)
        clear_sums()
        edge_pass(nc, "edges3", c, dram, res, dram["kv"].rearrange("t p f -> (t p) f"), dram["idx_src"], 2 * D, 8, True, False,
                  sums[:], q=q2)
        attention_output(nc, c, w, h[:], sums[:], q[:], h[:])
        batch_norm(nc, "bn1", c, w["L3_gnn_bn1_w"], w["L3_gnn_bn1_b"], h[:], square)
        with phase(nc, "copy3") as p:
            with nc.Block() as block:
                @block.vector
                def _(dve):
                    nc.vector.tensor_copy(q[:], h[:]).then_inc(p.sem("copied"), 1)
        feed_forward(nc, "ffn3", c, w["L3_gnn_W1"], w["L3_gnn_b1"], w["L3_gnn_W2"], w["L3_gnn_b2"], ACT.Relu, h[:], q[:])
        batch_norm(nc, "bn2", c, w["L3_gnn_bn2_w"], w["L3_gnn_bn2_b"], q[:], square, add_to=x[:])

        with phase(nc, "store") as p:
            stored = p.sem("stored")
            with nc.Block() as block:
                @block.sync
                def _(sp):
                    sp.dma_start(out[0:(NT - 1) * P].rearrange("(t p) d -> p t d", p=P), x[:, 0:NT - 1, :]).then_inc(stored, 16)
                    sp.dma_start(out[(NT - 1) * P:N], x[0:TAIL, NT - 1, :]).then_inc(stored, 16)
                    sp.wait_ge(stored, 32)


def for_rows(nc, name, gamma, beta, x, out, square, add=None):
    with phase(nc, name) as p:
        g, b = p.sb("gamma", [P, D]), p.sb("beta", [P, D])
        ln = LayerNorm(p, x, out, square, False, g[:], b[:])
        loaded = p.sem("loaded")
        with nc.Block() as block:
            @block.sync
            def _(sp):
                sp.dma_start(g[:], row_of(gamma)).then_inc(loaded, 16)
                sp.dma_start(b[:], row_of(beta)).then_inc(loaded, 16)

            @block.vector
            def _(dve):
                dve.wait_ge(loaded, 32)
                ln.vector(nc, dve)
                if add is not None:
                    nc.vector.tensor_tensor(add, add, x, ALU.add).then_inc(p.sem("added"), 1)

            @block.scalar
            def _(act):
                ln.scalar(nc, act)


def kernel(**inputs):
    import concourse.bacc as _bacc
    from concourse.bass_utils import run_bass_kernel_spmd as _run

    arrays = {k: np.ascontiguousarray(v) for k, v in inputs.items()}

    def nodes(a, fill=0):
        pad = np.full((NP - N,) + a.shape[1:], fill, a.dtype)
        return np.ascontiguousarray(np.concatenate([a, pad]).reshape((NT, P) + a.shape[1:]).swapaxes(0, 1))

    def groups(a, fill):
        return np.concatenate([a, np.full(((NG + 1) * GE - E,), fill, a.dtype)]).reshape(NG + 1, GE)

    arrays["x"] = nodes(arrays["x"])
    arrays["node_type_4"] = nodes(arrays["node_type_4"])
    arrays["dst"] = groups(arrays["dst"], NP - 1)
    arrays["src"] = groups(arrays["src"], NP - 1)
    arrays["edge_type_8"] = groups(arrays["edge_type_8"], 0)
    arrays["group_ends"] = np.ascontiguousarray(arrays["dst"][:NG, [0, GE - 1]].T)
    for name in ("L3_gnn_Wq", "L3_gnn_Wk", "L3_gnn_Wv", "L3_gnn_Wo", "L3_gnn_W1", "L3_gnn_W2"):
        arrays[name] = np.ascontiguousarray(arrays[name].T)
    for name in ("L1_gnn_b1", "L3_gnn_b1"):
        arrays[name] = np.ascontiguousarray(arrays[name].reshape(2, D).T)
    j = np.arange(P)
    consts = {
        "ident": np.eye(P, dtype=np.float32),
        "iota": np.arange(P, dtype=np.float32)[None],
        "ones_last": np.repeat((j < TAIL).astype(np.float32)[:, None], P, 1),
        "col_feat": np.stack([np.full(P, 128), np.ones(P), -2 * j, j * j // 128 * 128, j * j % 128]).astype(np.float32),
        "visit_ids": np.arange(NV, dtype=np.float32).reshape(VC, VP).T.copy(),
        "group_ids": np.arange(NG + 1, dtype=np.float32)[None],
    }
    nc = _bacc.Bacc("TRN2", target_bir_lowering=False, num_devices=1)
    feeds, w, cs = {}, {}, {}
    for pre, group, aps in (("in_", arrays, w), ("const_", consts, cs)):
        for name, a in group.items():
            feeds[pre + name] = a
            aps[name] = nc.dram_tensor(pre + name, a.shape, mybir.dt.from_np(a.dtype), kind="ExternalInput").ap()
    out = nc.dram_tensor("out_0_dram", (N, D), F32, kind="ExternalOutput").ap()
    graph_layers(nc, w, cs, out)
    r = _run(nc, [feeds], core_ids=[0])
    return r.results[0]["out_0_dram"]
```
